# Optimizing a Trainium2 kernel written in Bass

```python
import numpy as np
import jax
import jax.numpy as jnp

def _softmax(x, axis=-1):
    return jax.nn.softmax(x, axis=axis)

def _gelu(x):
    return jax.nn.gelu(x, approximate=True)

def _silu(x):
    return jax.nn.silu(x)

def _sigmoid(x):
    return jax.nn.sigmoid(x)

def _layernorm(x, axis=-1, eps=1e-05):
    m = jnp.mean(x, axis=axis, keepdims=True)
    v = jnp.var(x, axis=axis, keepdims=True)
    return (x - m) / jnp.sqrt(v + eps)

def _scatter_add(tgt, idx, src, axis=0):
    return tgt.at[idx].add(src)

def _segment_sum(src, seg, n):
    return jax.ops.segment_sum(src, seg, n)
kernel_name = 'mk_gnn_ffn_d1_gnn_r32_8a2679'

def setup_inputs(seed: int=0):
    np.random.seed(seed)
    _w = jnp.asarray

    def _rec_inputs():
        import jax
        import jax.numpy as jnp
        _gk = jax.random.key(seed)
        x = -0.0002117 + 1 * jax.random.normal(jax.random.fold_in(_gk, 1), (3125, 256), jnp.float32)
        _s = jax.random.randint(jax.random.fold_in(_gk, 2), (25000,), 0, 3125, jnp.int32)
        _d = jax.random.randint(jax.random.fold_in(_gk, 3), (25000,), 0, 3125, jnp.int32)
        _loop = jnp.arange(3125, dtype=jnp.int32)
        src = jnp.concatenate([_s, _d, _loop])
        dst = jnp.concatenate([_d, _s, _loop])
        _o = jnp.argsort(dst, stable=True)
        src = src[_o]
        dst = dst[_o]
        return (x, src, dst)
    x, src, dst = _rec_inputs()

    def _L0_gnn_setup():
        import jax, jax.numpy as jnp
        import numpy as np
        key = jax.random.key(seed)
        k1, k2, k3 = jax.random.split(key, 3)
        N, E, D_IN, D_OUT = (3125, 100000, 256, 256)
        x = jax.random.normal(k1, (N, D_IN), dtype=jnp.float32)
        W = jax.random.normal(k2, (D_OUT, D_IN), dtype=jnp.float32) * (1.0 / np.sqrt(D_IN))
        edge_index = jax.random.randint(k3, (2, E), 0, N, dtype=jnp.int32)
        return {'x': x, 'W': W, 'edge_index': edge_index}
    _L0_gnn_all = _L0_gnn_setup()
    _L0_gnn_in = {k: v for k, v in _L0_gnn_all.items() if k in ('W',)}
    del _L0_gnn_all

    def _L0_ffn_setup():
        import jax, jax.numpy as jnp
        import numpy as np
        NUM_EXPERTS = 8
        TOP_K = 2
        B, S, D = (8, 256, 256)

        def _moe(tokens, router_w, w1, b1, w2, b2):
            N = tokens.shape[0]
            E = router_w.shape[0]
            logits = tokens.astype(jnp.float32) @ router_w.astype(jnp.float32).T
            probs = jax.nn.softmax(logits, axis=-1)
            rw, re = jax.lax.top_k(probs, TOP_K)
            if TOP_K > 1:
                rw = rw / jnp.maximum(rw.sum(-1, keepdims=True), 1e-12)
            rw = rw.astype(tokens.dtype)
            combine = jnp.zeros((N, E), tokens.dtype).at[jnp.arange(N)[:, None], re].set(rw)
            out = tokens
            for e in range(E):
                h = jax.nn.gelu(tokens @ w1[e] + b1[e], approximate=False)
                y = h @ w2[e] + b2[e]
                out = out + combine[:, e:e + 1] * y
            return out
        key = jax.random.key(seed)
        ks = jax.random.split(key, 4)
        scale = 1.0 / np.sqrt(D).astype(np.float32)
        return {'input_embeddings': jax.random.normal(ks[0], (B, S, D), jnp.float32), 'router_w': jax.random.normal(ks[1], (NUM_EXPERTS, D), jnp.float32) * scale, 'w1': jax.random.normal(ks[2], (NUM_EXPERTS, D, D), jnp.float32) * scale, 'b1': jnp.zeros((NUM_EXPERTS, D), jnp.float32), 'w2': jax.random.normal(ks[3], (NUM_EXPERTS, D, D), jnp.float32) * scale, 'b2': jnp.zeros((NUM_EXPERTS, D), jnp.float32)}
    _L0_ffn_all = _L0_ffn_setup()
    _L0_ffn_in = {k: v for k, v in _L0_ffn_all.items() if k in ('router_w', 'w1', 'b1', 'w2', 'b2')}
    del _L0_ffn_all
    return {'x': x, 'src': src, 'dst': dst, 'L0_gnn_W': _L0_gnn_in['W'], 'L0_ffn_router_w': _L0_ffn_in['router_w'], 'L0_ffn_w1': _L0_ffn_in['w1'], 'L0_ffn_b1': _L0_ffn_in['b1'], 'L0_ffn_w2': _L0_ffn_in['w2'], 'L0_ffn_b2': _L0_ffn_in['b2']}

def reference(x, src, dst, L0_gnn_W, L0_ffn_router_w, L0_ffn_w1, L0_ffn_b1, L0_ffn_w2, L0_ffn_b2):
    import jax
    import jax.numpy as jnp

    def _L0_gnn_ref(x, W, edge_index):
        import jax, jax.numpy as jnp
        import numpy as np
        N = x.shape[0]
        loops = jnp.arange(N, dtype=edge_index.dtype)
        src = jnp.concatenate([edge_index[0], loops])
        dst = jnp.concatenate([edge_index[1], loops])
        deg = jax.ops.segment_sum(jnp.ones_like(src, dtype=x.dtype), src, num_segments=N)
        deg_rsqrt = jax.lax.rsqrt(deg)
        vals = deg_rsqrt[src] * deg_rsqrt[dst]
        h = x @ W.T
        msgs = vals[:, None] * h[dst]
        out = jax.ops.segment_sum(msgs, src, num_segments=N)
        return out

    def _L0_ffn_ref(input_embeddings, router_w, w1, b1, w2, b2):
        import jax, jax.numpy as jnp
        import numpy as np
        NUM_EXPERTS = 8
        TOP_K = 2
        B, S, D = (8, 256, 256)

        def _moe(tokens, router_w, w1, b1, w2, b2):
            N = tokens.shape[0]
            E = router_w.shape[0]
            logits = tokens.astype(jnp.float32) @ router_w.astype(jnp.float32).T
            probs = jax.nn.softmax(logits, axis=-1)
            rw, re = jax.lax.top_k(probs, TOP_K)
            if TOP_K > 1:
                rw = rw / jnp.maximum(rw.sum(-1, keepdims=True), 1e-12)
            rw = rw.astype(tokens.dtype)
            combine = jnp.zeros((N, E), tokens.dtype).at[jnp.arange(N)[:, None], re].set(rw)
            out = tokens
            for e in range(E):
                h = jax.nn.gelu(tokens @ w1[e] + b1[e], approximate=False)
                y = h @ w2[e] + b2[e]
                out = out + combine[:, e:e + 1] * y
            return out
        b, s, d = input_embeddings.shape
        tokens = input_embeddings.reshape(b * s, d)
        return _moe(tokens, router_w, w1, b1, w2, b2).reshape(b, s, d)
    edge_index = jnp.stack([src, dst])
    x = x + _L0_gnn_ref(_layernorm(x, axis=-1), L0_gnn_W, edge_index)
    x = x + _L0_ffn_ref(_layernorm(x, axis=-1)[None], L0_ffn_router_w, L0_ffn_w1, L0_ffn_b1, L0_ffn_w2, L0_ffn_b2)[0]
    return x

_drawn_inputs = setup_inputs


def setup_inputs(seed=0):
    import zlib

    import numpy as np

    out = dict(_drawn_inputs(seed))
    spreads = {'L0_ffn_b1': (0.0, 0.33), 'L0_ffn_b2': (0.0, 0.1)}
    factors = {}
    for name, (base, spread) in spreads.items():
        noise = np.random.default_rng([zlib.crc32(name.encode()), seed]).standard_normal(out[name].shape)
        drawn = base * np.exp(spread * noise) if base else spread * noise
        out[name] = jnp.asarray(drawn.astype(out[name].dtype))
    for name, factor in factors.items():
        out[name] = (out[name] * factor).astype(out[name].dtype)
    return out
```

```python
import concourse.bass as bass
from concourse import mybir
from contextlib import ExitStack

F32 = mybir.dt.float32
F16 = mybir.dt.float16
BF16 = mybir.dt.bfloat16
I32 = mybir.dt.int32
U32 = mybir.dt.uint32
ALU = mybir.AluOpType
ACT = mybir.ActivationFunctionType
AXX = mybir.AxisListType.X

P = 128


def gnn_moe(nc, x, src, dst, W, router_w, w1, b1, w2, b2, out):
    N, D = x.shape
    E = src.shape[0]
    NE = router_w.shape[0]
    KD = D // P
    NT = -(-N // P)
    NP = NT * P
    FULL = N // P
    TAIL = N - FULL * P
    GROUP = 16
    GPT = P // GROUP
    NG = NT * GPT
    J = 3
    WIN = J * P
    COLS = GROUP * NT
    BT = 5
    NB = NT // BT
    HG = NG // 2
    EC = 104
    EQ = 4
    NCH = EC * EQ
    EP = NCH * P
    TAB = EP + 4 * P
    PADNODE = NP
    PADVAL = float(PADNODE * NP + PADNODE)
    MAXR = -(-EP // WIN)
    RING = 4
    EPS = 1e-5
    CONSTS = 14
    assert NT % BT == 0 and NB % 2 == 1 and EP >= E and KD == 2 and NT * P == NP

    ctx = ExitStack()
    with ctx:
        def sb(name, shape, dt):
            return ctx.enter_context(nc.sbuf_tensor(name, shape, dt))

        def sem(name):
            return ctx.enter_context(nc.semaphore(name))

        X = sb("X", [P, NT, D], F32)
        identf = sb("identf", [P, P], F32)
        identh = sb("identh", [P, P], F16)
        WT = sb("WT", [P, KD, D], F32)
        rs = sb("rs", [P, NT], F32)
        rs2 = sb("rs2", [P, NT], F32)
        rsup = sb("rsup", [P, NT], F32)
        rsdown = sb("rsdown", [P, NT], F32)
        wmax = sb("wmax", [P, 2], F32)
        scaleb = sb("scaleb", [P, 2], F32)
        wtop = sb("wtop", [1, 4], F32)
        wexp = sb("wexp", [1, 1], I32)
        wpow = sb("wpow", [1, 2], I32)
        deg = sb("deg", [P, NT], F32)
        stats = sb("stats", [P, NT, 6], F32)
        mean = sb("mean", [P, NT], F32)
        rstd = sb("rstd", [P, NT], F32)
        lt1 = sb("lt1", [P, NT], F32)
        lt2 = sb("lt2", [P, NT], F32)
        xn = sb("xn", [P, 5, D], F32)
        xT = sb("xT", [P, 5, KD, P], F32)
        Wsb = xT[:, 0:KD, :, :].rearrange("p h k n -> p h (k n)")

        rw = xT[0:NE, KD, :, :].rearrange("p k n -> p (k n)")
        b1s = xT[0:NE, KD + 1, :, :].rearrange("p k n -> p (k n)")

        ARENA = 57600
        arena = sb("arena", [P, ARENA], F16)
        lowhot = arena[:, 0:P * NCH].rearrange("p (j c) -> p j c", c=NCH)
        AT = arena[:, 0:2 * NT * BT * P].rearrange("p (s a k c) -> p s a k c", s=2, a=NT, k=BT)
        o = 2 * NT * BT * P
        H = arena[:, o:o + 2 * NT * D].rearrange("p (s t d) -> p s t d", s=2, t=NT)
        o += 2 * NT * D
        CNT = arena[:, o:o + NT * P].rearrange("p (a d) -> p a d", a=NT)
        assert o + NT * P <= ARENA and P * NCH <= ARENA
        x2T = arena[:, 0:2 * KD * NP].bitcast(F32).rearrange("p (k n) -> p k n", k=KD)
        o = 2 * KD * NP
        hid = arena[:, o:o + 2 * 2 * KD * BT * P].bitcast(F32).rearrange("p (s k n) -> p s k n", s=2, k=KD)
        o += 2 * 2 * KD * BT * P
        w1s = arena[:, o:o + 2 * 2 * KD * D].bitcast(F32).rearrange("p (s k n) -> p s k n", s=2, k=KD)
        o += 2 * 2 * KD * D
        w2s = arena[:, o:o + 2 * 2 * KD * D].bitcast(F32).rearrange("p (s k n) -> p s k n", s=2, k=KD)
        assert o + 2 * 2 * KD * D <= ARENA

        wrows = sb("wrows", [P, 2, WIN], F32)
        SECOND = 43600
        second = sb("second", [P, SECOND // 2], F16)

        def lay(base, first, end):
            at = [first]

            def piece(rows, shape, dt):
                n = 1
                for d in shape:
                    n *= d
                size = n * (2 if dt == F16 else 4)
                v = base[0:rows, at[0] // 2:(at[0] + size) // 2]
                at[0] += size
                assert at[0] <= end
                v = v if dt == F16 else v.bitcast(dt)
                if len(shape) == 2:
                    v = v.rearrange("p (a b) -> p a b", b=shape[1])
                if len(shape) == 3:
                    v = v.rearrange("p (a b c) -> p a b c", b=shape[1], c=shape[2])
                return v
            return piece

        early = lay(second, 0, SECOND)
        esrc = early(EC, [EQ * P], I32)
        edst = early(EC, [EQ * P], I32)
        fsrc = early(EC, [EQ * P], F32)
        fdst = early(EC, [EQ * P], F32)
        eval_ = early(EC, [EQ * P], F32)
        wide = early(P, [EQ * P], F32)
        srcI = early(P, [NCH], I32)
        lowI = early(P, [NCH], I32)
        highI = early(P, [NCH], I32)
        lowh = early(P, [NCH], F16)
        highh = early(P, [NCH], F16)
        highhot = early(P, [NT, NCH], F16)
        cmpb = early(P, [NCH], F32)
        keytabf = early(P, [NT, GROUP], F32)
        kcmp = early(1, [MAXR], F32)
        late = lay(second, 0, SECOND)
        hself = late(P, [5, D], F32)
        aggs = late(P, [5, D], F32)
        hotlow = late(P, [RING, J, P], F16)
        hotkey = late(P, [RING, J, COLS], F16)
        winI = late(P, [J, NG], I32)
        lowwI = late(P, [J, NG], I32)
        keywI = late(P, [J, NG], I32)
        lowk = late(P, [J, NG], F32)
        key = late(P, [J, NG], F32)
        tail = lay(arena, 2 * P * NCH, 2 * ARENA)
        rowm = tail(1, [NCH], F32)
        rowp = tail(1, [NCH], F32)
        grow = tail(P, [2, P], F32)
        gscan = tail(P, [2, P], F32)
        bound = tail(1, [NG + 3 * EC], F32)
        diff = tail(1, [NG], F32)
        moe = lay(arena, 2 * (2 * KD * NP + 2 * 2 * KD * BT * P + 8 * KD * D), 2 * ARENA)
        b2s = moe(NE, [D], F32)
        logits = moe(P, [NT, NE], F32)
        probs = moe(P, [NT, NE], F32)
        comb = moe(P, [NT, NE], F32)
        top = moe(P, [NT, 8], F32)
        topf = moe(P, [NT, 2], F32)
        rowr = moe(P, [NT], F32)
        hot1 = moe(P, [NT, NE], F32)
        hot2 = moe(P, [NT, NE], F32)
        cring = moe(P, [5, NE], F32)
        cT = moe(NE, [5 * P], F32)
        b1e = moe(P, [2, KD], F32)
        topi = moe(P, [NT, 8], U32)

        padrow = sb("padrow", [1, TAB - EP], F32)
        unsorted = sb("unsorted", [EC, 1], F32)
        chmax = sb("chmax", [EC, EQ], F32)
        thrg = sb("thrg", [P, 2], F32)
        thr = sb("thr", [P, 2], F32)
        cg = sb("cg", [P, 2], F32)
        cgI = sb("cgI", [P, 2], I32)
        ng = sb("ng", [P, 2], F32)
        start = sb("start", [P, 2], F32)
        startc = sb("startc", [P, 2], F32)
        startI = sb("startI", [P, 2], I32)
        small = sb("small", [1, 8], F32)
        kwin = sb("kwin", [1, MAXR], F32)
        roundsI = sb("roundsI", [1, 1], I32)
        gbase = sb("gbase", [P, J, NG], F32)
        keytab = sb("keytab", [P, NT, GROUP], F16)
        iotaf = sb("iotaf", [P, P], F32)
        iotah = sb("iotah", [P, P], F16)
        ones = sb("ones", [1, P], F32)
        zerosh = sb("zerosh", [P, P], F16)

        rwT = sb("rwT", [P, KD, NE], F32)
        b1T = sb("b1T", [P, KD, NE], F32)
        iota8 = sb("iota8", [P, NT, NE], F32)

        lt3 = sb("lt3", [P, NT], F32)
        done = sb("done", [1, 1], F32)

        bank = [ctx.enter_context(nc.psum_tensor(f"bank{i}", [P, 512], F32)) for i in range(8)]

        edge_table = nc.dram_tensor("edge_table", [TAB, 1], F32, kind="Internal").ap()

        s_pad = sem("pads_written")
        s_edges = sem("edges_loaded")
        s_x = sem("x_loaded")
        s_w = sem("small_weights_loaded")
        s_b2 = sem("output_biases_loaded")
        s_const = sem("constants_ready")
        s_v = sem("vector_chain")
        s_val = sem("edge_values_ready")
        s_table = sem("edge_table_written")
        s_row = sem("chunk_rows_in_psum")
        s_mrow = sem("prefix_maxima_ready")
        s_mb = sem("prefix_maxima_spread")
        s_cg = sem("first_chunks_ready")
        s_grow = sem("first_chunks_gathered")
        s_start = sem("starts_ready")
        s_strow = sem("start_rows_in_psum")
        s_rounds = sem("rounds_ready")
        s_srcT = sem("sources_in_psum")
        s_hots = sem("source_onehots_ready")
        s_deg = sem("degrees_in_psum")
        s_sqrt = sem("sqrt_degree_ready")
        s_rs = sem("degree_scale_ready")
        s_wT = sem("weights_in_psum")
        s_wTc = sem("transposed_weights_ready")
        s_var = sem("variance_ready")
        s_std = sem("std_ready")
        s_xn = sem("normalised_rows_ready")
        s_tr = sem("row_transposes_in_psum")
        s_xT = sem("row_transposes_copied")
        s_h = sem("features_in_psum")
        s_hc = sem("features_split")
        s_hself = sem("self_loop_terms_copied")
        s_hadd = sem("self_loop_terms_added")
        s_wmax = sem("largest_weights_ready")
        s_wrow = sem("largest_weights_in_psum")
        s_ws = sem("feature_range_scale_ready")
        s_wb = sem("feature_range_scale_spread")
        s_p = sem("pool_chain")
        s_idx = sem("window_starts_ready")
        s_wg = sem("windows_gathered")
        s_wt = sem("windows_in_psum")
        s_key = sem("window_keys_ready")
        s_hot = sem("onehots_ready")
        s_cnt = sem("counts_in_psum")
        s_cc = sem("counts_copied")
        s_tp = sem("count_transposes_in_psum")
        s_tc = sem("count_transposes_copied")
        s_ag = sem("aggregates_in_psum")
        s_ac = sem("aggregates_copied")
        s_aa = sem("aggregates_added")
        s_b1e = sem("pair_biases_ready")
        s_window = sem("window_starts_seen")
        s_lg1 = sem("tile_logits_in_psum")
        s_round_end = sem("round_done")
        s_vr = sem("vector_chain_in_rounds")
        s_stat = sem("tile_statistics_done")
        s_x2 = sem("normalised_rows_kept")
        s_cring = sem("combine_rows_ready")
        s_lg = sem("logits_in_psum")
        s_lgc = sem("logits_copied")
        s_ex = sem("shifted_logits_ready")
        s_exd = sem("exponentials_ready")
        s_comb = sem("combine_ready")
        s_cT = sem("combine_transposes_in_psum")
        s_cTc = sem("combine_transposes_copied")
        s_bias = sem("bias_terms_in_psum")
        s_biasd = sem("bias_terms_added")
        s_ew = [sem(f"expert_weights_loaded{i}") for i in range(2)]
        s_hid = sem("hidden_in_psum")
        s_gelu = sem("hidden_ready")
        s_y = sem("expert_outputs_in_psum")
        s_yd = sem("expert_outputs_added")
        s_out = sem("outputs_written")

        block = ctx.enter_context(nc.Block())

        HR = 5
        CB = 2
        TB = 2
        AR = 5
        TPR = NT * BT
        AGR = NB * NT
        AB = NT // BT
        assert AB == BT == 5 and GPT == 8
        FREE_Y = 2 * BT
        HALFC = BT * P // 2
        AFTER_GROUP = {3: 0, 5: 1, 7: 2}
        AFTER_BATCH = {1: 3, 3: 4}

        EARLIER = [4, 0, 0, 0, 1]
        EXPO = float(127 + 15 + 126 - (D.bit_length() - 1))

        def half_slot(q):
            return bank[4 + q % 4][:, 0:D]

        def row_slot(q):
            return bank[q][:, 0:D]

        def feat_slot(q):
            return bank[q][:, D:2 * D]

        def feature_loop(eng, rows, features):
            AHEAD = 2
            for q in range(AHEAD):
                rows(0, q)
            with eng.Fori(0, NT // 5 - 1) as i:
                for q in range(5):
                    n = q + AHEAD
                    rows(i + n // 5 if n >= 5 else i, n % 5)
                    features(i, q)
            for q in range(5):
                if q + AHEAD < 5:
                    rows(NT // 5 - 1, q + AHEAD)
                features(NT // 5 - 1, q)

        def blocks(eng, r, step):
            with eng.Fori(0, BT) as k:
                step(r, k, 0, 0, None, None)
            with eng.Fori(0, (NB - 1) // 2) as i:
                for odd in range(2):
                    with eng.Fori(0, BT) as k:
                        step(r, k, i * 2 + (1 + odd), 1 - odd, i * 2 + odd, odd)
            with eng.Fori(0, BT) as k:
                step(r, k, None, None, NB - 1, 0)

        @block.sync
        def _(sp):
            whole = E // (EQ * P)
            rest = E - whole * EQ * P
            sp.wait_ge(s_pad, 3)
            for ten, dram in ((edst, dst), (esrc, src)):
                v = dram[0:whole * EQ * P].rearrange("(p c) -> p c", c=EQ * P)
                sp.dma_start(ten[0:96, :], v[0:96, :]).then_inc(s_edges, 16)
                sp.dma_start(ten[96:whole, :], v[96:whole, :]).then_inc(s_edges, 16)
                sp.dma_start(ten[whole:whole + 1, 0:rest],
                             dram[whole * EQ * P:E].rearrange("(p c) -> p c", p=1)).then_inc(s_edges, 16)
            sp.dma_start(Wsb, W.rearrange("(h p) c -> p h c", p=P)).then_inc(s_w, 16)
            sp.dma_start(rw, router_w).then_inc(s_w, 16)
            sp.dma_start(b1s, b1).then_inc(s_w, 16)
            for a in range(0, FULL, 6):
                sp.dma_start(X[:, a:a + 6, :],
                             x[a * P:(a + 6) * P, :].rearrange("(t p) c -> p t c", p=P)).then_inc(s_x, 16)
            cut = TAIL // 16 * 16
            sp.dma_start(X[0:cut, FULL, :], x[FULL * P:FULL * P + cut, :]).then_inc(s_x, 16)
            sp.dma_start(X[cut:TAIL, FULL, :], x[FULL * P + cut:N, :]).then_inc(s_x, 16)
            sp.wait_ge(s_val, 1)
            sp.wait_ge(s_const, 1)
            tab = edge_table.rearrange("n o -> (n o)")
            sp.dma_start(tab[0:EP].rearrange("(p c) -> p c", c=EQ * P), eval_[:]).then_inc(s_table, 16)
            sp.dma_start(tab[EP:TAB].rearrange("(p c) -> p c", p=1), padrow[:]).then_inc(s_table, 16)

            def load_expert(e, slot):
                for ten, dram in ((w1s, w1), (w2s, w2)):
                    sp.dma_start(ten[:, slot, :, :], dram[bass.ds(e, 1), :, :].rearrange(
                        "o (k p) c -> p (o k) c", p=P)).then_inc(s_ew[slot], 16)

            sp.wait_ge(s_round_end, 1)
            sp.dma_start(b2s[:], b2).then_inc(s_b2, 16)
            load_expert(0, 0)
            load_expert(1, 1)
            with sp.Fori(1, NE // 2) as i:
                for slot in range(2):
                    sp.wait_ge(s_y, FREE_Y + (i - 1) * (2 * NT) + (slot + 1) * NT)
                    load_expert(i * 2 + slot, slot)
            for t in range(0, FULL, 6):
                sp.wait_ge(s_yd, AR + (NE - 1) * NT + t + 6)
                sp.dma_start(out[t * P:(t + 6) * P, :].rearrange("(t p) c -> p t c", p=P),
                             X[:, t:t + 6, :]).then_inc(s_out, 16)
            sp.wait_ge(s_yd, AR + NE * NT)
            sp.dma_start(out[FULL * P:FULL * P + cut, :], X[0:cut, FULL, :]).then_inc(s_out, 16)
            sp.dma_start(out[FULL * P + cut:N, :], X[cut:TAIL, FULL, :]).then_inc(s_out, 16)
            sp.wait_ge(s_out, 16 * (FULL // 6 + 2))

        @block.gpsimd
        def _(pool):
            pool.memset(edst[96:EC, :], PADNODE).then_inc(s_pad, 1)
            pool.wait_ge(s_pad, 1)
            pool.memset(esrc[96:EC, :], PADNODE).then_inc(s_pad, 1)
            pool.wait_ge(s_pad, 2)
            pool.memset(X[:, FULL, :], 0.0).then_inc(s_pad, 1)
            pool.sem_inc(s_hadd, HR)
            pool.sem_inc(s_aa, AR)
            pool.sem_inc(s_x2, HR)
            n = [0]

            def const(ins):
                n[0] += 1
                ins.then_inc(s_const, 1)

            def iota(tile, pattern, mult):
                const(pool.iota(tile, pattern=pattern, base=0, channel_multiplier=mult,
                                allow_small_or_imprecise_dtypes=True))

            const(pool.memset(padrow[:], PADVAL))
            const(pool.memset(identf[:], 0.0))
            pool.wait_ge(s_const, n[0])
            const(pool.affine_select(out=identf[:], in_=identf[:], compare_op=ALU.not_equal, fill=1.0,
                                     base=0, pattern=[[-1, P]], channel_multiplier=1))
            const(pool.memset(ones[:], 1.0))
            const(pool.memset(zerosh[:], 0.0))
            iota(iotaf[:], [[1, P]], 0)
            iota(thrg[:], [[HG, 2]], 1)
            iota(kwin[:], [[WIN, MAXR]], 0)
            iota(keytabf[:], [[1, NT], [NT, GROUP]], 0)
            iota(gbase[:], [[0, J], [COLS, NG]], 0)
            iota(iota8[:], [[0, NT], [1, NE]], 0)
            pool.wait_ge(s_const, n[0])
            const(pool.tensor_copy(identh[:], identf[:]))
            const(pool.tensor_copy(iotah[:], iotaf[:]))
            const(pool.tensor_copy(keytab[:], keytabf[:]))
            assert n[0] == CONSTS

            rows = edge_table.rearrange("(a b) o -> a (b o)", b=P)
            pool.wait_ge(s_table, 32)
            pool.wait_ge(s_cg, 1)
            for h in range(2):
                pool.indirect_dma_start(grow[0:HG, h, :], None, rows,
                                        bass.IndirectOffsetOnAxis(cgI[0:HG, h:h + 1], 0)).then_inc(s_grow, 16)

            def gather_windows():
                for h in range(2):
                    pool.indirect_dma_start(wrows[0:HG, h, :], None, edge_table,
                                            bass.IndirectOffsetOnAxis(startI[0:HG, h:h + 1], 0)).then_inc(s_wg, 16)

            pool.wait_ge(s_idx, 1)
            gather_windows()
            with pool.Fori(0, NT // 5) as i:
                for q in range(5):
                    t = i * 5 + q
                    pool.wait_ge(s_hself, t + 1 + HR)
                    xt = X[:, bass.ds(t, 1), :].rearrange("p o d -> p (o d)")
                    pool.tensor_tensor(xt, xt, hself[:, q, :], ALU.add).then_inc(s_hadd, 1)

            R = pool.value_load(roundsI[0:1, 0:1], min_val=1, max_val=MAXR)
            with pool.Fori(0, R) as r:
                pool.wait_ge(s_idx, r + 2)
                pool.wait_ge(s_wt, r + 1)
                pool.sem_inc(s_window, 1)
                gather_windows()
                with pool.Fori(0, NB) as b:
                    with pool.Fori(0, BT) as k:
                        for q in range(BT):
                            pool.wait_ge(s_ac, r * AGR + b * NT + k * BT + (q + AR + 1))
                            xt = X[:, bass.ds(k * BT + q, 1), :].rearrange("p o d -> p (o d)")
                            pool.tensor_tensor(xt, xt, aggs[:, q, :], ALU.add).then_inc(s_aa, 1)
            pool.wait_ge(s_wg, R * 32 + 32)
            pool.sem_inc(s_window, 1)
            pool.memset(done[:], 0.0).then_inc(s_round_end, 1)

            with pool.Fori(0, NT // 5) as i:
                for q in range(5):
                    t = i * 5 + q
                    pool.wait_ge(s_xT, NT + t + 1)
                    pool.tensor_copy(x2T[:, :, bass.ds(t * P, P)], xT[:, q, :, :])
                    xt = X[:, bass.ds(t, 1), :].rearrange("p o d -> p (o d)")
                    pool.tensor_tensor(xt, xt, xn[:, q, :], ALU.add).then_inc(s_x2, 1)

        @block.scalar
        def _(act):
            act.sem_inc(s_cc, CB)
            act.sem_inc(s_tc, TB)
            act.sem_inc(s_ac, AR)
            act.sem_inc(s_gelu, 4)
            act.sem_inc(s_hself, HR)
            act.wait_ge(s_wT, 1)
            act.activation(WT[:], bank[5][:, :].rearrange("p (k n) -> p k n", k=KD), ACT.Copy).then_inc(s_wTc, 1)
            act.activation(rwT[:], bank[6][:, 0:KD * NE].rearrange("p (k n) -> p k n", k=KD), ACT.Copy).then_inc(s_wTc, 1)
            act.activation(b1T[:], bank[6][:, 64:64 + KD * NE].rearrange("p (k n) -> p k n", k=KD),
                           ACT.Copy).then_inc(s_wTc, 1)
            act.wait_ge(s_var, 1)
            act.activation(lt2[:], lt1[:], ACT.Sqrt).then_inc(s_std, 1)
            act.wait_ge(s_deg, 1)
            act.activation(deg[:], bank[7][:, 0:NT], ACT.Sqrt, bias=1.0).then_inc(s_sqrt, 1)

            def copy_rows(i, q):
                act.wait_ge(s_tr, i * 5 + (q + 1 + HR))
                act.activation(xT[:, q, :, :], row_slot(q).rearrange("p (k n) -> p k n", k=KD),
                               ACT.Copy).then_inc(s_xT, 1)

            def copy_features(i, q):
                t = i * 5 + q
                act.wait_ge(s_rs, 1)
                act.wait_ge(s_h, t + 1)
                act.activation(H[:, 0, bass.ds(t, 1), :].rearrange("p o d -> p (o d)"), feat_slot(q),
                               ACT.Copy, scale=rsup[:, bass.ds(t, 1)])
                act.wait_ge(s_rs, 1)
                act.wait_ge(s_hadd, t + 1)
                act.activation(hself[:, q, :], feat_slot(q), ACT.Copy, scale=rs2[:, bass.ds(t, 1)]).then_inc(s_hself, 1)

            act.wait_ge(s_rs, 1)
            feature_loop(act, copy_rows, copy_features)

            def step(r, k, bb, slot, ab, aslot):
                def aggregate(q):
                    n = r * AGR + ab * NT + k * BT + (q + 1)
                    act.wait_ge(s_rs, 1)
                    act.wait_ge(s_ag, n)
                    act.wait_ge(s_aa, n)
                    act.activation(aggs[:, q, :], half_slot(q), ACT.Copy,
                                   scale=rsdown[:, bass.ds(k * BT + q, 1)]).then_inc(s_ac, 1)

                if bb is None:
                    for q in range(BT):
                        aggregate(q)
                    return
                for g in range(GPT):
                    n = r * NG + bb * (BT * GPT) + k * GPT + (g + 1)
                    act.wait_ge(s_cnt, n + RING)
                    act.activation(CNT[:, :, g * GROUP:(g + 1) * GROUP],
                                   bank[g % CB][:, 0:COLS].rearrange("p (a d) -> p a d", a=NT),
                                   ACT.Copy).then_inc(s_cc, 1)
                    if ab is not None and g in AFTER_GROUP:
                        aggregate(AFTER_GROUP[g])
                for b in range(BT):
                    n = r * TPR + bb * (BT * BT) + k * BT + (b + 1)
                    act.wait_ge(s_deg, 1)
                    act.wait_ge(s_tp, n)
                    act.activation(AT[:, slot, b * AB:(b + 1) * AB, bass.ds(k, 1), :].rearrange("p a o c -> p a (o c)"),
                                   bank[2 + b % TB][:, :].bitcast(F16)[:, 0:AB * P].rearrange("p (a c) -> p a c", a=AB),
                                   ACT.Copy).then_inc(s_tc, 1)
                    if ab is not None and b in AFTER_BATCH:
                        aggregate(AFTER_BATCH[b])

            act.wait_ge(s_rounds, 1)
            R = act.value_load(roundsI[0:1, 0:1], min_val=1, max_val=MAXR)
            with act.Fori(0, R) as r:
                blocks(act, r, step)

            act.wait_ge(s_var, 2)
            act.activation(lt2[:], lt1[:], ACT.Sqrt).then_inc(s_std, 1)
            with act.Fori(0, NT // 5) as i:
                for q in range(5):
                    t = i * 5 + q
                    act.wait_ge(s_tr, NT + t + 1 + HR)
                    act.wait_ge(s_x2, t + 1)
                    act.activation(xT[:, q, :, :], row_slot(q).rearrange("p (k n) -> p k n", k=KD),
                                   ACT.Copy).then_inc(s_xT, 1)
            act.wait_ge(s_ex, 1)
            act.activation(probs[:], logits[:], ACT.Exp).then_inc(s_exd, 1)
            with act.Fori(0, NT // 5) as i:
                act.wait_ge(s_cT, i + 1)
                act.activation(cT[:, 0:3 * P], bank[5][0:NE, 0:3 * P], ACT.Copy)
                act.activation(cT[:, 3 * P:5 * P], bank[6][0:NE, 0:2 * P], ACT.Copy).then_inc(s_cTc, 1)
            with act.Fori(0, NE // 2) as i:
                act.wait_ge(s_gelu, i * (8 * NB) + 4)
                act.activation(b1e[:], b1T[:, :, bass.ds(i * 2, 2)].rearrange("p f e -> p e f"), ACT.Copy).then_inc(s_b1e, 1)
                act.wait_ge(s_b1e, i + 1)
                for m in range(2 * NB):
                    act.wait_ge(s_y, i * (2 * NT) + (m * BT + BT))
                    for u in range(4):
                        act.wait_ge(s_hid, i * (8 * NB) + (m * 4 + u + 1))
                        f, th = u // 2, u % 2
                        act.activation(hid[:, m % 2, f, th * HALFC:(th + 1) * HALFC], bank[u][:, 0:HALFC],
                                       ACT.Gelu, bias=b1e[:, m // NB, f:f + 1]).then_inc(s_gelu, 1)

        @block.vector
        def _(dve):
            dve.sem_inc(s_yd, AR)
            dve.sem_inc(s_hc, HR)
            count = [0]

            def link(ins):
                count[0] += 1
                ins.then_inc(s_v, 1)
                dve.wait_ge(s_v, count[0])

            dve.wait_ge(s_edges, 96)
            dve.tensor_copy(fdst[:], edst[:])
            link(dve.tensor_copy(fsrc[:], esrc[:]))
            dve.scalar_tensor_tensor(eval_[:], fdst[:], float(NP), fsrc[:], ALU.mult, ALU.add).then_inc(s_val, 1)
            dve.wait_ge(s_val, 1)
            dve.tensor_reduce(chmax[:], eval_[:].rearrange("p (q e) -> p q e", q=EQ), AXX, ALU.max).then_inc(s_val, 1)
            L = EQ * P - 1
            link(dve.tensor_tensor(wide[0:EC, 0:L], fdst[:, 0:L], fdst[:, 1:L + 1], ALU.is_gt))
            link(dve.tensor_reduce(unsorted[:], wide[0:EC, 0:L], AXX, ALU.add))
            dve.wait_ge(s_row, 1)
            link(dve.tensor_copy(rowm[:].rearrange("o (p q) -> o q p", q=EQ),
                                 bank[0][0:1, 0:NCH].rearrange("o (q p) -> o q p", q=EQ)))
            dve.tensor_tensor_scan(rowp[:], rowm[:], rowm[:], 0.0, ALU.max, ALU.max).then_inc(s_mrow, 1)
            dve.wait_ge(s_mb, 1)
            dve.wait_ge(s_const, CONSTS)
            link(dve.tensor_scalar(thr[:], thrg[:], float(GROUP * NP), None, ALU.mult))
            for h in range(2):
                link(dve.tensor_scalar(cmpb[0:HG, :], bank[1][0:HG, 0:NCH], thr[0:HG, h:h + 1], None, ALU.is_lt))
                link(dve.tensor_reduce(cg[0:HG, h:h + 1], cmpb[0:HG, :], AXX, ALU.add))
            dve.tensor_copy(cgI[0:HG, :], cg[0:HG, :]).then_inc(s_cg, 1)

            dve.wait_ge(s_w, 48)
            dve.tensor_reduce(wmax[:, 0:1], Wsb.rearrange("p h c -> p (h c)"), AXX, ALU.max).then_inc(s_wmax, 1)
            dve.tensor_reduce(wmax[:, 1:2], Wsb.rearrange("p h c -> p (h c)"), AXX, ALU.min).then_inc(s_wmax, 1)

            dve.wait_ge(s_srcT, 1)
            link(dve.tensor_copy(srcI[:], bank[2][:, 0:NCH]))
            dve.tensor_scalar(lowI[:], srcI[:], P - 1, None, ALU.bitwise_and)
            link(dve.tensor_scalar(highI[:], srcI[:], 7, None, ALU.arith_shift_right))
            dve.tensor_copy(lowh[:], lowI[:])
            link(dve.tensor_copy(highh[:], highI[:]))
            with dve.Fori(0, NT // 5) as i:
                for u in range(5):
                    j = i * 5 + u
                    dve.tensor_scalar(highhot[:, bass.ds(j, 1), :].rearrange("p o c -> p (o c)"), highh[:],
                                      iotaf[:, bass.ds(j, 1)], None, ALU.is_equal).then_inc(s_hots, 1)
            dve.wait_ge(s_wrow, 1)
            dve.tensor_reduce(wtop[:, 0:1], bank[3][0:1, 0:P], AXX, ALU.max)
            link(dve.tensor_reduce(wtop[:, 1:2], bank[3][0:1, P:2 * P], AXX, ALU.min))
            link(dve.tensor_scalar(wtop[:, 1:2], wtop[:, 1:2], -1.0, None, ALU.mult))
            link(dve.tensor_tensor(wtop[:, 0:1], wtop[:, 0:1], wtop[:, 1:2], ALU.max))
            link(dve.tensor_scalar(wexp[:], wtop[:, 0:1].bitcast(I32), 23, None, ALU.arith_shift_right))
            link(dve.tensor_copy(wtop[:, 1:2], wexp[:]))
            link(dve.tensor_scalar(wtop[:, 2:3], wtop[:, 1:2], -1.0, EXPO, ALU.mult, ALU.add))
            link(dve.tensor_scalar(wtop[:, 2:3], wtop[:, 2:3], 253.0, float(1 << 23), ALU.min, ALU.mult))
            link(dve.tensor_scalar(wtop[:, 3:4], wtop[:, 2:3], -1.0, 254.0 * (1 << 23), ALU.mult, ALU.add))
            dve.tensor_copy(wpow[:], wtop[:, 2:4]).then_inc(s_ws, 1)
            with dve.Fori(0, P // 8) as i:
                for u in range(8):
                    j = i * 8 + u
                    dve.tensor_scalar(lowhot[:, bass.ds(j, 1), :].rearrange("p o c -> p (o c)"), lowh[:],
                                      iotaf[:, bass.ds(j, 1)], None, ALU.is_equal).then_inc(s_hots, 1)

            dve.wait_ge(s_wb, 1)
            link(dve.tensor_copy(scaleb[:], bank[4][:, 0:2]))

            dve.wait_ge(s_grow, 32)
            for h in range(2):
                link(dve.tensor_tensor_scan(gscan[0:HG, h, :], grow[0:HG, h, :], grow[0:HG, h, :], 0.0, ALU.max, ALU.max))
                link(dve.tensor_scalar(cmpb[0:HG, 0:P], gscan[0:HG, h, :], thr[0:HG, h:h + 1], None, ALU.is_lt))
                link(dve.tensor_reduce(ng[0:HG, h:h + 1], cmpb[0:HG, 0:P], AXX, ALU.add))
            dve.scalar_tensor_tensor(start[0:HG, :], cg[0:HG, :], float(P), ng[0:HG, :], ALU.mult, ALU.add).then_inc(s_start, 1)
            dve.wait_ge(s_start, 1)
            link(dve.tensor_copy(startc[0:HG, :], start[0:HG, :]))
            dve.tensor_copy(startI[0:HG, :], startc[0:HG, :]).then_inc(s_idx, 1)
            dve.wait_ge(s_strow, 1)
            link(dve.tensor_copy(bound[:], bank[0][0:1, 0:NG + 3 * EC]))
            link(dve.tensor_tensor(diff[:, 0:NG - 1], bound[:, 1:NG], bound[:, 0:NG - 1], ALU.subtract))
            dve.tensor_reduce(small[:, 0:1], diff[:, 0:NG - 1], AXX, ALU.max)
            link(dve.tensor_tensor(rowm[:, 0:EC - 1], bound[:, NG:NG + EC - 1], bound[:, NG + EC + 1:NG + 2 * EC], ALU.is_gt))
            dve.tensor_reduce(small[:, 1:2], rowm[:, 0:EC - 1], AXX, ALU.add)
            link(dve.tensor_reduce(small[:, 2:3], bound[:, NG + 2 * EC:NG + 3 * EC], AXX, ALU.add))
            link(dve.tensor_tensor(small[:, 3:4], small[:, 1:2], small[:, 2:3], ALU.add))
            link(dve.tensor_scalar(small[:, 4:5], small[:, 3:4], 0.0, float(EP), ALU.is_gt, ALU.mult))
            link(dve.tensor_tensor(small[:, 5:6], small[:, 4:5], small[:, 0:1], ALU.max))
            link(dve.tensor_scalar(kcmp[:], kwin[:], small[:, 5:6], None, ALU.is_lt))
            link(dve.tensor_reduce(small[:, 6:7], kcmp[:], AXX, ALU.add))
            link(dve.tensor_scalar(small[:, 7:8], small[:, 6:7], 1.0, None, ALU.max))
            dve.tensor_copy(roundsI[:], small[:, 7:8]).then_inc(s_rounds, 1)

            def layernorm(base):
                with dve.Fori(0, NT // 5) as i:
                    for u in range(5):
                        t = i * 5 + u
                        dve.bn_stats(stats[:, bass.ds(t, 1), :].rearrange("p o s -> p (o s)"),
                                     X[:, bass.ds(t, 1), :].rearrange("p o d -> p (o d)")).then_inc(s_stat, 1)
                dve.wait_ge(s_stat, base * NT + NT)
                me, mo, ve, vo = (stats[:, :, c] for c in (1, 4, 2, 5))
                dve.tensor_tensor(lt1[:], me, mo, ALU.add)
                link(dve.tensor_tensor(lt2[:], me, mo, ALU.subtract))
                dve.tensor_scalar(mean[:], lt1[:], 0.5, None, ALU.mult)
                dve.tensor_tensor(rstd[:], ve, vo, ALU.add)
                link(dve.scalar_tensor_tensor(lt3[:], lt2[:], 0.25, lt2[:], ALU.mult, ALU.mult))
                link(dve.scalar_tensor_tensor(lt2[:], rstd[:], 1.0 / D, lt3[:], ALU.mult, ALU.add))
                dve.tensor_scalar(lt1[:], lt2[:], EPS, None, ALU.add).then_inc(s_var, 1)
                dve.wait_ge(s_std, base + 1)
                link(dve.reciprocal(rstd[:], lt2[:]))

            def normalise(base, i, q):
                t = i * 5 + q
                dve.wait_ge(s_tr, base * NT + t + 1)
                if base:
                    dve.wait_ge(s_x2, t + 1)
                xt = X[:, bass.ds(t, 1), :].rearrange("p o d -> p (o d)")
                dve.tensor_scalar(xn[:, q, :], xt, mean[:, bass.ds(t, 1)], rstd[:, bass.ds(t, 1)],
                                  ALU.subtract, ALU.mult).then_inc(s_xn, 1)

            def split_features(i, q):
                t = i * 5 + q
                dve.wait_ge(s_hself, t + 1 + HR)
                part = H[:, :, bass.ds(t, 1), :].rearrange("p s o d -> p s (o d)")
                dve.scalar_tensor_tensor(part[:, 1, :], feat_slot(q), rsup[:, bass.ds(t, 1)], part[:, 0, :],
                                         ALU.mult, ALU.subtract).then_inc(s_hc, 1)

            dve.wait_ge(s_x, 16 * (FULL // 6 + 2))
            layernorm(0)
            dve.wait_ge(s_sqrt, 1)
            link(dve.reciprocal(rs[:], deg[:]))
            dve.tensor_tensor(rs2[:], rs[:], rs[:], ALU.mult)
            dve.tensor_scalar(rsdown[:], rs[:], scaleb[:, 1:2], None, ALU.mult)
            dve.tensor_scalar(rsup[:], rs[:], scaleb[:, 0:1], None, ALU.mult).then_inc(s_rs, 1)
            dve.wait_ge(s_rs, 1)
            for q in range(5):
                normalise(0, 0, q)
            with dve.Fori(0, NT // 5 - 1) as i:
                for q in range(5):
                    split_features(i, q)
                    normalise(0, i + 1, q)
            for q in range(5):
                split_features(NT // 5 - 1, q)

            R = dve.value_load(roundsI[0:1, 0:1], min_val=1, max_val=MAXR)
            KR = 3

            with dve.Fori(0, R) as r:
                def rlink(ins, n):
                    ins.then_inc(s_vr, 1)
                    dve.wait_ge(s_vr, r * KR + n)

                rlink(dve.tensor_scalar(startc[0:HG, :], startc[0:HG, :], float(WIN), float(EP), ALU.add, ALU.min), 1)
                dve.wait_ge(s_wg, r * 32 + 32)
                dve.tensor_copy(startI[0:HG, :], startc[0:HG, :]).then_inc(s_idx, 1)
                dve.wait_ge(s_wt, r + 1)
                dve.tensor_copy(winI[:, 0:2, :], bank[2][:, 0:2 * NG].rearrange("p (j g) -> p j g", j=2))
                rlink(dve.tensor_copy(winI[:, 2:3, :], bank[3][:, 0:NG].rearrange("p (j g) -> p j g", j=1)), 2)
                dve.tensor_scalar(lowwI[:], winI[:], P - 1, None, ALU.bitwise_and)
                rlink(dve.tensor_scalar(keywI[:], winI[:], 7, None, ALU.arith_shift_right), 3)
                dve.tensor_copy(lowk[:], lowwI[:])
                dve.tensor_tensor(key[:], keywI[:], gbase[:], ALU.subtract).then_inc(s_key, 1)
                dve.wait_ge(s_sqrt, 1)
                dve.wait_ge(s_key, r + 1)
                with dve.Fori(0, NT) as t:
                    for g in range(GPT):
                        col = t * GPT + g
                        dve.wait_ge(s_cnt, r * NG + t * GPT + (g + 1))
                        for j in range(J):
                            dve.tensor_scalar(hotlow[:, g % RING, j, :], iotah[:], lowk[:, j, bass.ds(col, 1)],
                                              None, ALU.is_equal)
                            last = dve.tensor_scalar(hotkey[:, g % RING, j, :], keytab[:].rearrange("p a d -> p (a d)"),
                                                     key[:, j, bass.ds(col, 1)], None, ALU.is_equal)
                        last.then_inc(s_hot, 1)

            dve.wait_ge(s_round_end, 1)
            layernorm(1)
            with dve.Fori(0, NT // 5) as i:
                for q in range(5):
                    normalise(1, i, q)
            dve.wait_ge(s_lg, 1)
            link(dve.tensor_copy(logits[:], bank[7][:, 0:NT * NE].rearrange("p (t e) -> p t e", t=NT)))
            link(dve.tensor_reduce(rowr[:], logits[:], AXX, ALU.max))
            wide8 = lambda a: a.unsqueeze(2).to_broadcast([P, NT, NE])
            dve.tensor_tensor(logits[:], logits[:], wide8(rowr[:]), ALU.subtract).then_inc(s_ex, 1)
            dve.wait_ge(s_exd, 1)
            link(dve.tensor_reduce(rowr[:], probs[:], AXX, ALU.add))
            link(dve.reciprocal(lt1[:], rowr[:]))
            link(dve.tensor_tensor(probs[:], probs[:], wide8(lt1[:]), ALU.mult))
            for t in range(NT):
                last = dve.max(top[:, t, :], probs[:, t, :])
            link(last)
            for t in range(NT):
                last = dve.max_index(topi[:, t, :], top[:, t, :], probs[:, t, :])
            link(last)
            link(dve.tensor_copy(topf[:], topi[:, :, 0:2]))
            link(dve.tensor_tensor(lt1[:], top[:, :, 0], top[:, :, 1], ALU.add))
            link(dve.tensor_scalar(lt2[:], lt1[:], 1e-12, None, ALU.max))
            dve.reciprocal(rowr[:], lt2[:])
            dve.tensor_tensor(hot1[:], iota8[:], wide8(topf[:, :, 0]), ALU.is_equal)
            link(dve.tensor_tensor(hot2[:], iota8[:], wide8(topf[:, :, 1]), ALU.is_equal))
            link(dve.tensor_tensor(hot1[:], hot1[:], hot2[:], ALU.add))
            link(dve.tensor_tensor(hot1[:], hot1[:], probs[:], ALU.mult))
            link(dve.tensor_tensor(comb[:], hot1[:], wide8(rowr[:]), ALU.mult))
            dve.wait_ge(s_x2, NT + HR)
            with dve.Fori(0, NT // 5) as i:
                for q in range(5):
                    ins = dve.tensor_copy(cring[:, q, :], comb[:, bass.ds(i * 5 + q, 1), :].rearrange("p o e -> p (o e)"))
                ins.then_inc(s_cring, 1)
                for q in range(5):
                    t = i * 5 + q
                    dve.wait_ge(s_bias, t + 1)
                    xt = X[:, bass.ds(t, 1), :].rearrange("p o d -> p (o d)")
                    dve.tensor_tensor(xt, xt, row_slot(q), ALU.add).then_inc(s_biasd, 1)
            dve.wait_ge(s_biasd, NT)
            with dve.Fori(0, NE // 2) as i:
                for m in range(2 * NB):
                    for q in range(BT):
                        dve.wait_ge(s_y, i * (2 * NT) + (m * BT + q + 1 + FREE_Y))
                        t = (m % NB) * BT + q
                        dve.scalar_tensor_tensor(X[:, t, :], half_slot(q),
                                                 comb[:, t, bass.ds(i * 2 + m // NB, 1)], X[:, t, :],
                                                 ALU.mult, ALU.add).then_inc(s_yd, 1)

        @block.tensor
        def _(pe):
            mm = pe.matmul
            pe.sem_inc(s_cnt, RING)
            pe.sem_inc(s_tr, HR)
            pe.sem_inc(s_y, FREE_Y)
            pe.wait_ge(s_const, CONSTS)
            pe.wait_ge(s_val, 2)
            for q in range(EQ):
                last = mm(bank[0][0:1, q * EC:(q + 1) * EC], chmax[:, q:q + 1], identf[0:EC, 0:EC], start=True, stop=True)
            last.then_inc(s_row, 1)
            for q in range(EQ):
                last = pe.transpose(bank[2][:, q * EC:(q + 1) * EC], fsrc[:, q * P:(q + 1) * P], identf[0:EC, 0:EC])
            last.then_inc(s_srcT, 1)
            pe.wait_ge(s_mrow, 1)
            mm(bank[1][:, 0:NCH], ones[:], rowp[:], start=True, stop=True).then_inc(s_mb, 1)
            pe.wait_ge(s_w, 48)
            for k in range(KD):
                for h in range(KD):
                    pe.transpose(bank[5][:, k * D + h * P:k * D + (h + 1) * P], Wsb[:, h, k * P:(k + 1) * P], identf[:])
            for k in range(KD):
                pe.transpose(bank[6][:, k * NE:(k + 1) * NE], rw[:, k * P:(k + 1) * P], identf[0:NE, 0:NE])
                last = pe.transpose(bank[6][:, 64 + k * NE:64 + (k + 1) * NE], b1s[:, k * P:(k + 1) * P], identf[0:NE, 0:NE])
            last.then_inc(s_wT, 1)
            pe.wait_ge(s_wmax, 2)
            for m in range(2):
                last = mm(bank[3][0:1, m * P:(m + 1) * P], wmax[:, m:m + 1], identf[:], start=True, stop=True)
            last.then_inc(s_wrow, 1)
            pe.wait_ge(s_ws, 1)
            mm(bank[4][:, 0:2], ones[:], wpow[:].bitcast(F32), start=True, stop=True).then_inc(s_wb, 1)
            pe.wait_ge(s_start, 1)
            for h in range(2):
                mm(bank[0][0:1, h * HG:(h + 1) * HG], start[0:HG, h:h + 1], identf[0:HG, 0:HG], start=True, stop=True)
            for n, col in enumerate((fdst[:, EQ * P - 1:EQ * P], fdst[:, 0:1], unsorted[:])):
                last = mm(bank[0][0:1, NG + n * EC:NG + (n + 1) * EC], col, identf[0:EC, 0:EC], start=True, stop=True)
            last.then_inc(s_strow, 1)
            pe.wait_ge(s_hots, NT + P)
            mm(bank[7][:, 0:NT], zerosh[:], zerosh[:, 0:NT], start=True, stop=False)
            for c in range(NCH):
                mm(bank[7][:, 0:NT], lowhot[:, :, c], highhot[:, :, c], start=False, stop=False)
            mm(bank[7][:, 0:NT], zerosh[:], zerosh[:, 0:NT], start=False, stop=True).then_inc(s_deg, 1)

            def transpose_rows(base, i, q):
                pe.wait_ge(s_xn, base * NT + i * 5 + (q + 1))
                for k in range(KD):
                    last = pe.transpose(row_slot(q)[:, k * P:(k + 1) * P], xn[:, q, k * P:(k + 1) * P], identf[:])
                last.then_inc(s_tr, 1)

            def rows(i, q):
                pe.wait_ge(s_hc, i * 5 + (q + 1))
                transpose_rows(0, i, q)

            def features(i, q):
                pe.wait_ge(s_xT, i * 5 + (q + 1))
                for k in range(KD):
                    last = mm(feat_slot(q), xT[:, q, k, :], WT[:, k, :], start=(k == 0), stop=(k == KD - 1))
                last.then_inc(s_h, 1)

            pe.wait_ge(s_wTc, 3)
            pe.wait_ge(s_rounds, 1)
            pe.wait_ge(s_wb, 1)
            feature_loop(pe, rows, features)

            def step(r, k, bb, slot, ab, aslot):
                def aggregate(q):
                    n = r * AGR + ab * NT + k * BT + (q + 1)
                    pe.wait_ge(s_ac, n + EARLIER[q])
                    for j in range(BT):
                        for s in range(2):
                            last = mm(half_slot(q),
                                      AT[:, aslot, bass.ds(k * BT + q, 1), j, :].rearrange("p o c -> p (o c)"),
                                      H[:, s, bass.ds(ab * BT + j, 1), :].rearrange("p o d -> p (o d)"),
                                      start=(j == 0 and s == 0), stop=(j == BT - 1 and s == 1))
                    last.then_inc(s_ag, 1)

                if ab is not None:
                    pe.wait_ge(s_tc, r * TPR + ab * NT + (NT + TB))
                if bb is None:
                    for q in range(BT):
                        aggregate(q)
                    return
                for g in range(GPT):
                    n = r * NG + bb * (BT * GPT) + k * GPT + (g + 1)
                    pe.wait_ge(s_hot, n)
                    pe.wait_ge(s_cc, n)
                    for j in range(J):
                        last = mm(bank[g % CB][:, 0:COLS], hotlow[:, g % RING, j, :], hotkey[:, g % RING, j, :],
                                  start=(j == 0), stop=(j == J - 1))
                    last.then_inc(s_cnt, 1)
                    if ab is not None and g in AFTER_GROUP:
                        aggregate(AFTER_GROUP[g])
                pe.wait_ge(s_cc, r * NG + bb * (BT * GPT) + k * GPT + (GPT + CB))
                for b in range(BT):
                    n = r * TPR + bb * NT + k * BT + (b + 1)
                    pe.wait_ge(s_tc, n + (1 if b == 0 else 0))
                    for u in range(AB):
                        last = pe.transpose(bank[2 + b % TB][:, :].bitcast(F16)[:, u * P:(u + 1) * P],
                                            CNT[:, b * AB + u, :], identh[:])
                    last.then_inc(s_tp, 1)
                    if ab is not None and b in AFTER_BATCH:
                        aggregate(AFTER_BATCH[b])

            pe.wait_ge(s_hc, NT + HR)
            R = pe.value_load(roundsI[0:1, 0:1], min_val=1, max_val=MAXR)
            with pe.Fori(0, R) as r:
                pe.wait_ge(s_wg, r * 32 + 32)
                pe.wait_ge(s_tc, r * TPR + TB)
                for j in range(J):
                    for h in range(2):
                        c = (j % 2) * NG + h * HG
                        last = pe.transpose(bank[2 + j // 2][:, c:c + HG], wrows[0:HG, h, j * P:(j + 1) * P],
                                            identf[0:HG, 0:HG])
                last.then_inc(s_wt, 1)
                blocks(pe, r, step)

            def route(i, q):
                pe.wait_ge(s_xT, NT + i * 5 + (q + 1))
                for k in range(KD):
                    last = mm(bank[7][:, bass.ds(i * (5 * NE) + q * NE, NE)], xT[:, q, k, :], rwT[:, k, :],
                              start=(k == 0), stop=(k == KD - 1))
                last.then_inc(s_lg1, 1)

            pe.wait_ge(s_round_end, 1)
            with pe.Fori(0, NT // 5) as i:
                transpose_rows(1, i, 0)
                for q in range(1, 5):
                    transpose_rows(1, i, q)
                    route(i, q - 1)
                route(i, 4)
            mm(bank[6][:, 0:8], zerosh[:], zerosh[:, 0:8], start=True, stop=True).then_inc(s_lg, 1)
            pe.wait_ge(s_b2, 16)
            with pe.Fori(0, NT // 5) as i:
                pe.wait_ge(s_cring, i + 1)
                for q in range(5):
                    b, c = (5, q * P) if q < 3 else (6, (q - 3) * P)
                    last = pe.transpose(bank[b][0:NE, c:c + P], cring[:, q, :], identf[:])
                last.then_inc(s_cT, 1)
                pe.wait_ge(s_cTc, i + 1)
                for q in range(5):
                    mm(row_slot(q), cT[:, q * P:(q + 1) * P], b2s[:], start=True, stop=True).then_inc(s_bias, 1)

            def hidden(i, m):
                slot, c = m // NB, m % NB
                if c == 0:
                    pe.wait_ge(s_ew[slot], i * 32 + 32)
                for u in range(4):
                    f, th = u // 2, u % 2
                    pe.wait_ge(s_gelu, i * (8 * NB) + (m * 4 + u + 1))
                    for k in range(KD):
                        last = mm(bank[u][:, 0:HALFC], w1s[:, slot, k, f * P:(f + 1) * P],
                                  x2T[:, k, c * BT * P + th * HALFC:c * BT * P + (th + 1) * HALFC],
                                  start=(k == 0), stop=(k == KD - 1))
                    last.then_inc(s_hid, 1)

            def outputs(i, m):
                slot = m // NB
                pe.wait_ge(s_gelu, i * (8 * NB) + (m * 4 + 4 + 4))
                for q in range(BT):
                    pe.wait_ge(s_yd, i * (2 * NT) + (m * BT + q + 1 + EARLIER[q]))
                    for k in range(KD):
                        last = mm(half_slot(q), hid[:, m % 2, k, q * P:(q + 1) * P], w2s[:, slot, k, :],
                                  start=(k == 0), stop=(k == KD - 1))
                    last.then_inc(s_y, 1)

            pe.wait_ge(s_biasd, NT)
            with pe.Fori(0, NE // 2) as i:
                hidden(i, 0)
                for m in range(2 * NB):
                    if m + 1 < 2 * NB:
                        hidden(i, m + 1)
                    outputs(i, m)


_INS = ["x", "src", "dst", "L0_gnn_W", "L0_ffn_router_w", "L0_ffn_w1", "L0_ffn_b1", "L0_ffn_w2", "L0_ffn_b2"]


def kernel(**inputs):
    import numpy as _np
    import concourse.bacc as _bacc
    from concourse import mybir as _mybir
    from concourse.bass_utils import run_bass_kernel_spmd as _run

    nc = _bacc.Bacc("TRN2", target_bir_lowering=False, num_devices=1)
    arrays, args = {}, []
    for name in _INS:
        a = _np.ascontiguousarray(inputs[name])
        arrays[f"in_{name}"] = a
        args.append(nc.dram_tensor(f"in_{name}", a.shape, _mybir.dt.from_np(a.dtype), kind="ExternalInput").ap())
    shape = inputs["x"].shape
    args.append(nc.dram_tensor("out", shape, _mybir.dt.float32, kind="ExternalOutput").ap())
    gnn_moe(nc, *args)
    r = _run(nc, [arrays], core_ids=[0])
    return r.results[0]["out"]
```

```python
import concourse.bass as bass
from concourse import mybir
from contextlib import ExitStack

F32 = mybir.dt.float32
F16 = mybir.dt.float16
I32 = mybir.dt.int32
U32 = mybir.dt.uint32
ALU = mybir.AluOpType
ACT = mybir.ActivationFunctionType
AXX = mybir.AxisListType.X

P = 128


def gnn_moe(nc, x, src, dst, W, router_w, w1, b1, w2, b2, out):
    N, D = x.shape
    E = src.shape[0]
    NE = router_w.shape[0]
    KD = D // P
    NT = -(-N // P)
    NP = NT * P
    FULL = N // P
    TAIL = N - FULL * P
    GROUP = 16
    GPT = P // GROUP
    NG = NT * GPT
    J = 3
    WIN = J * P
    COLS = GROUP * NT
    BT = 5
    NB = NT // BT
    HG = NG // 2
    EC = 104
    EQ = 4
    NCH = EC * EQ
    EP = NCH * P
    TAB = EP + 4 * P
    PADNODE = NP
    PADVAL = float(PADNODE * NP + PADNODE)
    MAXR = -(-EP // WIN)
    RING = 4
    EPS = 1e-5
    CONSTS = 15
    assert NT % BT == 0 and NB % 2 == 1 and EP >= E and KD == 2 and NT * P == NP

    ctx = ExitStack()
    with ctx:
        def sb(name, shape, dt):
            return ctx.enter_context(nc.sbuf_tensor(name, shape, dt))

        def sem(name):
            return ctx.enter_context(nc.semaphore(name))

        X = sb("X", [P, NT, D], F32)
        identf = sb("identf", [P, P], F32)
        identh = sb("identh", [P, P], F16)
        WT = sb("WT", [P, KD, D], F32)
        rs = sb("rs", [P, NT], F32)
        rs2 = sb("rs2", [P, NT], F32)
        rsup = sb("rsup", [P, NT], F32)
        rsdown = sb("rsdown", [P, NT], F32)
        wmax = sb("wmax", [P, 2], F32)
        emax = sb("emax", [P, 2, 2 * NE], F32)
        etop = sb("etop", [2 * NE, 4], F32)
        eexp = sb("eexp", [2 * NE, 2], I32)
        epow = sb("epow", [2 * NE, 4], I32)
        ediag = sb("ediag", [2 * NE, 4, 2 * NE], F32)
        bmax = sb("bmax", [2 * NE, 2], F32)
        scaleb = sb("scaleb", [P, 2], F32)
        wtop = sb("wtop", [1, 4], F32)
        wexp = sb("wexp", [1, 1], I32)
        wpow = sb("wpow", [1, 2], I32)
        deg = sb("deg", [P, NT], F32)
        stats = sb("stats", [P, NT, 6], F32)
        mean = sb("mean", [P, NT], F32)
        rstd = sb("rstd", [P, NT], F32)
        lt1 = sb("lt1", [P, NT], F32)
        lt2 = sb("lt2", [P, NT], F32)
        xn = sb("xn", [P, 5, D], F32)
        xT = sb("xT", [P, 5, KD, P], F32)
        Wsb = xT[:, 0:KD, :, :].rearrange("p h k n -> p h (k n)")

        rw = xT[0:NE, KD, :, :].rearrange("p k n -> p (k n)")
        b1s = xT[0:NE, KD + 1, :, :].rearrange("p k n -> p (k n)")

        ARENA = 57600
        arena = sb("arena", [P, ARENA], F16)
        lowhot = arena[:, 0:P * NCH].rearrange("p (j c) -> p j c", c=NCH)
        AT = arena[:, 0:2 * NT * BT * P].rearrange("p (s a k c) -> p s a k c", s=2, a=NT, k=BT)
        o = 2 * NT * BT * P
        H = arena[:, o:o + 2 * NT * D].rearrange("p (s t d) -> p s t d", s=2, t=NT)
        o += 2 * NT * D
        CNT = arena[:, o:o + NT * P].rearrange("p (a d) -> p a d", a=NT)
        assert o + NT * P <= ARENA and P * NCH <= ARENA
        taken = [0]

        def half(parts, cols):
            taken[0] += parts * cols
            return arena[:, taken[0] - parts * cols:taken[0]]

        x2 = half(2 * KD, NP).rearrange("p (s k n) -> p s k n", s=2, k=KD)
        hid = half(4 * KD, BT * P).rearrange("p (s m k n) -> p s m k n", s=2, m=2, k=KD)
        hidf = half(2 * 4, BT * P // 2).bitcast(F32).rearrange("p (u n) -> p u n", u=4)
        wparts = half(2 * 2 * 2 * KD, D).rearrange("p (m s o w) -> p m s o w", m=2, s=2, o=2)
        MOE = 2 * taken[0]
        wrows = sb("wrows", [P, 2, WIN], F32)
        SECOND = 43600
        second = sb("second", [P, SECOND // 2], F16)

        def lay(base, first, end):
            at = [first]

            def piece(rows, shape, dt):
                n = 1
                for d in shape:
                    n *= d
                size = n * (2 if dt == F16 else 4)
                v = base[0:rows, at[0] // 2:(at[0] + size) // 2]
                at[0] += size
                assert at[0] <= end
                v = v if dt == F16 else v.bitcast(dt)
                if len(shape) == 2:
                    v = v.rearrange("p (a b) -> p a b", b=shape[1])
                if len(shape) == 3:
                    v = v.rearrange("p (a b c) -> p a b c", b=shape[1], c=shape[2])
                return v
            return piece

        early = lay(second, 0, SECOND)
        esrc = early(EC, [EQ * P], I32)
        edst = early(EC, [EQ * P], I32)
        fsrc = early(EC, [EQ * P], F32)
        fdst = early(EC, [EQ * P], F32)
        eval_ = early(EC, [EQ * P], F32)
        wide = early(P, [EQ * P], F32)
        srcI = early(P, [NCH], I32)
        lowI = early(P, [NCH], I32)
        highI = early(P, [NCH], I32)
        lowh = early(P, [NCH], F16)
        highh = early(P, [NCH], F16)
        highhot = early(P, [NT, NCH], F16)
        cmpb = early(P, [NCH], F32)
        keytabf = early(P, [NT, GROUP], F32)
        kcmp = early(1, [MAXR], F32)
        late = lay(second, 0, SECOND)
        aggs = late(P, [5, D], F32)
        wf = second[:, 5 * D * 2:5 * D * 2 + 2 * NE * 2 * KD * D].bitcast(F32).rearrange(
            "p (e o w) -> p e o w", e=NE, o=2)
        assert (5 * D + NE * 2 * KD * D) * 4 <= SECOND
        hself = late(P, [5, D], F32)
        hotlow = late(P, [RING, J, P], F16)
        hotkey = late(P, [RING, J, COLS], F16)
        winI = late(P, [J, NG], I32)
        lowwI = late(P, [J, NG], I32)
        keywI = late(P, [J, NG], I32)
        lowk = late(P, [J, NG], F32)
        key = late(P, [J, NG], F32)
        tail = lay(arena, 2 * P * NCH, 2 * ARENA)
        rowm = tail(1, [NCH], F32)
        rowp = tail(1, [NCH], F32)
        grow = tail(P, [2, P], F32)
        gscan = tail(P, [2, P], F32)
        bound = tail(1, [NG + 3 * EC], F32)
        diff = tail(1, [NG], F32)
        moe = lay(arena, MOE, 2 * ARENA)
        b2s = moe(NE, [D], F32)
        logits = moe(P, [NT, NE], F32)
        probs = moe(P, [NT, NE], F32)
        comb = moe(P, [NT, NE], F32)
        top = moe(P, [NT, 8], F32)
        topf = moe(P, [NT, 2], F32)
        rowr = moe(P, [NT], F32)
        hot1 = moe(P, [NT, NE], F32)
        hot2 = moe(P, [NT, NE], F32)
        combs = moe(P, [NT, NE], F32)
        cT = moe(NE, [NT * P], F32)
        b1e = moe(P, [2, KD], F32)
        spread = moe(P, [4, 2 * NE], F32)
        gdown = moe(P, [NE], F32)
        ydown = moe(P, [NE], F32)
        hup = moe(P, [2, 1], F32)
        gel = moe(P, [2, 1], F32)
        wup = moe(P, [2, 2], F32)
        topi = moe(P, [NT, 8], U32)

        padrow = sb("padrow", [1, TAB - EP], F32)
        unsorted = sb("unsorted", [EC, 1], F32)
        chmax = sb("chmax", [EC, EQ], F32)
        thrg = sb("thrg", [P, 2], F32)
        thr = sb("thr", [P, 2], F32)
        cg = sb("cg", [P, 2], F32)
        cgI = sb("cgI", [P, 2], I32)
        ng = sb("ng", [P, 2], F32)
        start = sb("start", [P, 2], F32)
        startc = sb("startc", [P, 2], F32)
        startI = sb("startI", [P, 2], I32)
        small = sb("small", [1, 8], F32)
        kwin = sb("kwin", [1, MAXR], F32)
        roundsI = sb("roundsI", [1, 1], I32)
        gbase = sb("gbase", [P, J, NG], F32)
        keytab = sb("keytab", [P, NT, GROUP], F16)
        iotaf = sb("iotaf", [P, P], F32)
        iotah = sb("iotah", [P, P], F16)
        ones = sb("ones", [2 * NE, P], F32)
        zerosh = sb("zerosh", [P, P], F16)

        rwT = sb("rwT", [P, KD, NE], F32)
        b1T = sb("b1T", [P, KD, NE], F32)
        iota8 = sb("iota8", [P, NT, NE], F32)

        lt3 = sb("lt3", [P, NT], F32)
        done = sb("done", [1, 1], F32)

        bank = [ctx.enter_context(nc.psum_tensor(f"bank{i}", [P, 512], F32)) for i in range(8)]

        edge_table = nc.dram_tensor("edge_table", [TAB, 1], F32, kind="Internal").ap()

        s_pad = sem("pads_written")
        s_edges = sem("edges_loaded")
        s_x = sem("x_loaded")
        s_w = sem("small_weights_loaded")
        s_b2 = sem("output_biases_loaded")
        s_const = sem("constants_ready")
        s_v = sem("vector_chain")
        s_val = sem("edge_values_ready")
        s_table = sem("edge_table_written")
        s_row = sem("chunk_rows_in_psum")
        s_mrow = sem("prefix_maxima_ready")
        s_mb = sem("prefix_maxima_spread")
        s_cg = sem("first_chunks_ready")
        s_grow = sem("first_chunks_gathered")
        s_start = sem("starts_ready")
        s_strow = sem("start_rows_in_psum")
        s_rounds = sem("rounds_ready")
        s_srcT = sem("sources_in_psum")
        s_hots = sem("source_onehots_ready")
        s_deg = sem("degrees_in_psum")
        s_sqrt = sem("sqrt_degree_ready")
        s_rs = sem("degree_scale_ready")
        s_wT = sem("weights_in_psum")
        s_wTc = sem("transposed_weights_ready")
        s_var = sem("variance_ready")
        s_sum = sem("row_sums_ready")
        s_std = sem("std_ready")
        s_xn = sem("normalised_rows_ready")
        s_tr = sem("row_transposes_in_psum")
        s_xT = sem("row_transposes_copied")
        s_h = sem("features_in_psum")
        s_hc = sem("features_split")
        s_hself = sem("self_loop_terms_copied")
        s_hadd = sem("self_loop_terms_added")
        s_wmax = sem("largest_weights_ready")
        s_wrow = sem("largest_weights_in_psum")
        s_ws = sem("feature_range_scale_ready")
        s_wb = sem("feature_range_scale_spread")
        s_idx = sem("window_starts_ready")
        s_wg = sem("windows_gathered")
        s_wt = sem("windows_in_psum")
        s_key = sem("window_keys_ready")
        s_hot = sem("onehots_ready")
        s_cnt = sem("counts_in_psum")
        s_cc = sem("counts_copied")
        s_tp = sem("count_transposes_in_psum")
        s_tc = sem("count_transposes_copied")
        s_ag = sem("aggregates_in_psum")
        s_ac = sem("aggregates_copied")
        s_aa = sem("aggregates_added")
        s_b1e = sem("pair_biases_ready")
        s_window = sem("window_starts_seen")
        s_lg1 = sem("tile_logits_in_psum")
        s_round_end = sem("round_done")
        s_vr = sem("vector_chain_in_rounds")
        s_stat = sem("tile_statistics_done")
        s_x2 = sem("normalised_rows_kept")
        s_lg = sem("logits_in_psum")
        s_ex = sem("shifted_logits_ready")
        s_exd = sem("exponentials_ready")
        s_comb = sem("combine_ready")
        s_cT = sem("combine_transposes_in_psum")
        s_cTc = sem("combine_transposes_copied")
        s_bias = sem("bias_terms_in_psum")
        s_biasd = sem("bias_terms_added")
        s_ew = sem("expert_weights_loaded")
        s_emax = sem("largest_expert_weights_ready")
        s_erow = sem("largest_expert_weights_in_psum")
        s_epow = sem("powers_of_two_ready")
        s_espread = sem("powers_of_two_in_psum")
        s_es = sem("powers_of_two_copied")
        s_whi = sem("first_weight_parts_ready")
        s_wlo = sem("second_weight_parts_ready")
        s_xhi = sem("first_row_parts_ready")
        s_xlo = sem("second_row_parts_ready")
        s_hhi = sem("first_hidden_parts_ready")
        s_hlo = sem("second_hidden_parts_ready")
        s_hid = sem("hidden_in_psum")
        s_gelu = sem("hidden_ready")
        s_y = sem("expert_outputs_in_psum")
        s_yd = sem("expert_outputs_added")
        s_out = sem("outputs_written")

        block = ctx.enter_context(nc.Block())

        HR = 5
        CB = 2
        TB = 2
        AR = 5
        TPR = NT * BT
        AGR = NB * NT
        AB = NT // BT
        assert AB == BT == 5 and GPT == 8
        FREE_Y = 2 * BT
        HALFC = BT * P // 2
        AFTER_GROUP = {3: 0, 5: 1, 7: 2}
        AFTER_BATCH = {1: 3, 3: 4}

        EARLIER = [4, 0, 0, 0, 1]
        XUP = float(1 << 11)
        CTB = -(-NT // 4)
        YB = -(-NT // 2)
        BOUND_EXP = float(127 + 15 + 126)
        FEATURE_EXP = BOUND_EXP - (D.bit_length() - 1)

        def half_slot(q):
            return bank[4 + q % 4][:, 0:D]

        def row_slot(q):
            return bank[q][:, 0:D]

        def feat_slot(q):
            return bank[q][:, D:2 * D]

        def feature_loop(eng, rows, features):
            AHEAD = 2
            for q in range(AHEAD):
                rows(0, q)
            with eng.Fori(0, NT // 5 - 1) as i:
                for q in range(5):
                    n = q + AHEAD
                    rows(i + n // 5 if n >= 5 else i, n % 5)
                    features(i, q)
            for q in range(5):
                if q + AHEAD < 5:
                    rows(NT // 5 - 1, q + AHEAD)
                features(NT // 5 - 1, q)

        def blocks(eng, r, step):
            with eng.Fori(0, BT) as k:
                step(r, k, 0, 0, None, None)
            with eng.Fori(0, (NB - 1) // 2) as i:
                for odd in range(2):
                    with eng.Fori(0, BT) as k:
                        step(r, k, i * 2 + (1 + odd), 1 - odd, i * 2 + odd, odd)
            with eng.Fori(0, BT) as k:
                step(r, k, None, None, NB - 1, 0)

        @block.sync
        def _(sp):
            whole = E // (EQ * P)
            rest = E - whole * EQ * P
            sp.wait_ge(s_pad, 3)
            for ten, dram in ((edst, dst), (esrc, src)):
                v = dram[0:whole * EQ * P].rearrange("(p c) -> p c", c=EQ * P)
                sp.dma_start(ten[0:96, :], v[0:96, :]).then_inc(s_edges, 16)
                sp.dma_start(ten[96:whole, :], v[96:whole, :]).then_inc(s_edges, 16)
                sp.dma_start(ten[whole:whole + 1, 0:rest],
                             dram[whole * EQ * P:E].rearrange("(p c) -> p c", p=1)).then_inc(s_edges, 16)
            sp.dma_start(Wsb, W.rearrange("(h p) c -> p h c", p=P)).then_inc(s_w, 16)
            sp.dma_start(rw, router_w).then_inc(s_w, 16)
            sp.dma_start(b1s, b1).then_inc(s_w, 16)
            for a in range(0, FULL, 6):
                sp.dma_start(X[:, a:a + 6, :],
                             x[a * P:(a + 6) * P, :].rearrange("(t p) c -> p t c", p=P)).then_inc(s_x, 16)
            cut = TAIL // 16 * 16
            sp.dma_start(X[0:cut, FULL, :], x[FULL * P:FULL * P + cut, :]).then_inc(s_x, 16)
            sp.dma_start(X[cut:TAIL, FULL, :], x[FULL * P + cut:N, :]).then_inc(s_x, 16)
            sp.wait_ge(s_val, 1)
            sp.wait_ge(s_const, 1)
            tab = edge_table.rearrange("n o -> (n o)")
            sp.dma_start(tab[0:EP].rearrange("(p c) -> p c", c=EQ * P), eval_[:]).then_inc(s_table, 16)
            sp.dma_start(tab[EP:TAB].rearrange("(p c) -> p c", p=1), padrow[:]).then_inc(s_table, 16)

            sp.wait_ge(s_rounds, 1)
            R = sp.value_load(roundsI[0:1, 0:1], min_val=1, max_val=MAXR)
            sp.wait_ge(s_cnt, R * NG + RING)
            def load_expert(e):
                for o, dram in enumerate((w1, w2)):
                    sp.dma_start(wf[:, bass.ds(e, 1), o, :].rearrange("p a (k c) -> p (a k) c", k=KD),
                                 dram[bass.ds(e, 1), :, :].rearrange("a (k p) c -> p (a k) c", p=P)).then_inc(s_ew, 16)

            load_expert(0)
            with sp.Fori(1, NE) as e:
                load_expert(e)
            sp.wait_ge(s_round_end, 1)
            sp.dma_start(b2s[:], b2).then_inc(s_b2, 16)
            for t in range(0, FULL, 6):
                sp.wait_ge(s_yd, AR + (NE - 1) * NT + t + 6)
                sp.dma_start(out[t * P:(t + 6) * P, :].rearrange("(t p) c -> p t c", p=P),
                             X[:, t:t + 6, :]).then_inc(s_out, 16)
            sp.wait_ge(s_yd, AR + NE * NT)
            sp.dma_start(out[FULL * P:FULL * P + cut, :], X[0:cut, FULL, :]).then_inc(s_out, 16)
            sp.dma_start(out[FULL * P + cut:N, :], X[cut:TAIL, FULL, :]).then_inc(s_out, 16)
            sp.wait_ge(s_out, 16 * (FULL // 6 + 2))

        @block.gpsimd
        def _(pool):
            pool.memset(edst[96:EC, :], PADNODE).then_inc(s_pad, 1)
            pool.wait_ge(s_pad, 1)
            pool.memset(esrc[96:EC, :], PADNODE).then_inc(s_pad, 1)
            pool.wait_ge(s_pad, 2)
            pool.memset(X[:, FULL, :], 0.0).then_inc(s_pad, 1)
            pool.sem_inc(s_hadd, HR)
            pool.sem_inc(s_aa, AR + NT)
            pool.sem_inc(s_x2, HR)
            n = [0]

            def const(ins):
                n[0] += 1
                ins.then_inc(s_const, 1)

            def iota(tile, pattern, mult):
                const(pool.iota(tile, pattern=pattern, base=0, channel_multiplier=mult,
                                allow_small_or_imprecise_dtypes=True))

            const(pool.memset(padrow[:], PADVAL))
            const(pool.memset(identf[:], 0.0))
            pool.wait_ge(s_const, n[0])
            const(pool.affine_select(out=identf[:], in_=identf[:], compare_op=ALU.not_equal, fill=1.0,
                                     base=0, pattern=[[-1, P]], channel_multiplier=1))
            const(pool.memset(ones[:], 1.0))
            const(pool.memset(bmax[:], 0.0))
            const(pool.memset(zerosh[:], 0.0))
            iota(iotaf[:], [[1, P]], 0)
            iota(thrg[:], [[HG, 2]], 1)
            iota(kwin[:], [[WIN, MAXR]], 0)
            iota(keytabf[:], [[1, NT], [NT, GROUP]], 0)
            iota(gbase[:], [[0, J], [COLS, NG]], 0)
            iota(iota8[:], [[0, NT], [1, NE]], 0)
            pool.wait_ge(s_const, n[0])
            const(pool.tensor_copy(identh[:], identf[:]))
            const(pool.tensor_copy(iotah[:], iotaf[:]))
            const(pool.tensor_copy(keytab[:], keytabf[:]))
            assert n[0] == CONSTS

            rows = edge_table.rearrange("(a b) o -> a (b o)", b=P)
            pool.wait_ge(s_table, 32)
            pool.wait_ge(s_cg, 1)
            for h in range(2):
                pool.indirect_dma_start(grow[0:HG, h, :], None, rows,
                                        bass.IndirectOffsetOnAxis(cgI[0:HG, h:h + 1], 0)).then_inc(s_grow, 16)

            def gather_windows():
                for h in range(2):
                    pool.indirect_dma_start(wrows[0:HG, h, :], None, edge_table,
                                            bass.IndirectOffsetOnAxis(startI[0:HG, h:h + 1], 0)).then_inc(s_wg, 16)

            pool.wait_ge(s_idx, 1)
            gather_windows()
            with pool.Fori(0, NT // 5) as i:
                for q in range(5):
                    t = i * 5 + q
                    pool.wait_ge(s_hself, t + 1 + HR)
                    xt = X[:, bass.ds(t, 1), :].rearrange("p o d -> p (o d)")
                    pool.tensor_tensor(xt, xt, hself[:, q, :], ALU.add).then_inc(s_hadd, 1)

            R = pool.value_load(roundsI[0:1, 0:1], min_val=1, max_val=MAXR)
            with pool.Fori(0, R) as r:
                pool.wait_ge(s_idx, r + 2)
                pool.wait_ge(s_wt, r + 1)
                pool.sem_inc(s_window, 1)
                gather_windows()
                with pool.Fori(0, NB) as b:
                    with pool.Fori(0, BT) as k:
                        for q in range(BT):
                            pool.wait_ge(s_ac, r * AGR + b * NT + k * BT + (q + AR + 1))
                            xt = X[:, bass.ds(k * BT + q, 1), :].rearrange("p o d -> p (o d)")
                            pool.tensor_tensor(xt, xt, aggs[:, q, :], ALU.add).then_inc(s_aa, 1)
            pool.wait_ge(s_wg, R * 32 + 32)
            pool.sem_inc(s_window, 1)
            pool.memset(done[:], 0.0).then_inc(s_round_end, 1)

            with pool.Fori(0, NT // 5) as i:
                for q in range(5):
                    t = i * 5 + q
                    pool.wait_ge(s_xn, NT + t + 1)
                    xt = X[:, bass.ds(t, 1), :].rearrange("p o d -> p (o d)")
                    pool.tensor_tensor(xt, xt, xn[:, q, :], ALU.add).then_inc(s_x2, 1)

        @block.scalar
        def _(act):
            act.sem_inc(s_cc, CB)
            act.sem_inc(s_tc, TB)
            act.sem_inc(s_ac, AR)
            act.sem_inc(s_gelu, 4)
            act.sem_inc(s_hself, HR)
            act.sem_inc(s_xhi, HR)
            act.sem_inc(s_sum, 5)
            act.wait_ge(s_wT, 1)
            act.activation(WT[:], bank[5][:, :].rearrange("p (k n) -> p k n", k=KD), ACT.Copy).then_inc(s_wTc, 1)
            act.activation(rwT[:], bank[6][:, 0:KD * NE].rearrange("p (k n) -> p k n", k=KD), ACT.Copy).then_inc(s_wTc, 1)
            act.activation(b1T[:], bank[6][:, 64:64 + KD * NE].rearrange("p (k n) -> p k n", k=KD),
                           ACT.Copy).then_inc(s_wTc, 1)
            act.wait_ge(s_x, 16 * (FULL // 6 + 2))
            for t in range(NT):
                act.wait_ge(s_sum, t + 1)
                act.activation(xn[:, t % 5, :], X[:, t, :], ACT.Copy, accum_out=lt1[:, t:t + 1]).then_inc(s_sum, 1)
            act.wait_ge(s_sum, NT + 5)
            act.activation(lt3[:], lt1[:], ACT.Copy, scale=-1.0 / D).then_inc(s_sum, 1)
            act.wait_ge(s_sum, NT + 6)
            for t in range(NT):
                act.wait_ge(s_sum, NT + t + 2)
                act.activation(xn[:, t % 5, :], X[:, t, :], ACT.Square, bias=lt3[:, t:t + 1],
                               accum_out=lt2[:, t:t + 1]).then_inc(s_sum, 1)
            act.wait_ge(s_sum, 2 * NT + 6)
            act.activation(lt1[:], lt2[:], ACT.Copy, scale=1.0 / D, bias=EPS).then_inc(s_var, 1)
            act.wait_ge(s_var, 1)
            act.activation(lt2[:], lt1[:], ACT.Sqrt).then_inc(s_std, 1)
            act.wait_ge(s_deg, 1)
            act.activation(deg[:], bank[7][:, 0:NT], ACT.Sqrt, bias=1.0).then_inc(s_sqrt, 1)

            def copy_rows(i, q):
                act.wait_ge(s_tr, i * 5 + (q + 1 + HR))
                act.activation(xT[:, q, :, :], row_slot(q).rearrange("p (k n) -> p k n", k=KD),
                               ACT.Copy).then_inc(s_xT, 1)

            def copy_features(i, q):
                t = i * 5 + q
                act.wait_ge(s_rs, 1)
                act.wait_ge(s_h, t + 1)
                act.activation(H[:, 0, bass.ds(t, 1), :].rearrange("p o d -> p (o d)"), feat_slot(q),
                               ACT.Copy, scale=rsup[:, bass.ds(t, 1)])
                act.wait_ge(s_rs, 1)
                act.wait_ge(s_hadd, t + 1)
                act.activation(hself[:, q, :], feat_slot(q), ACT.Copy, scale=rs2[:, bass.ds(t, 1)]).then_inc(s_hself, 1)

            act.wait_ge(s_rs, 1)
            feature_loop(act, copy_rows, copy_features)

            def step(r, k, bb, slot, ab, aslot):
                def aggregate(q):
                    n = r * AGR + ab * NT + k * BT + (q + 1)
                    act.wait_ge(s_rs, 1)
                    act.wait_ge(s_ag, n)
                    act.wait_ge(s_aa, n + NT)
                    act.activation(aggs[:, q, :], half_slot(q), ACT.Copy,
                                   scale=rsdown[:, bass.ds(k * BT + q, 1)]).then_inc(s_ac, 1)

                if bb is None:
                    for q in range(BT):
                        aggregate(q)
                    return
                for g in range(GPT):
                    n = r * NG + bb * (BT * GPT) + k * GPT + (g + 1)
                    act.wait_ge(s_cnt, n + RING)
                    act.activation(CNT[:, :, g * GROUP:(g + 1) * GROUP],
                                   bank[g % CB][:, 0:COLS].rearrange("p (a d) -> p a d", a=NT),
                                   ACT.Copy).then_inc(s_cc, 1)
                    if ab is not None and g in AFTER_GROUP:
                        aggregate(AFTER_GROUP[g])
                for b in range(BT):
                    n = r * TPR + bb * (BT * BT) + k * BT + (b + 1)
                    act.wait_ge(s_deg, 1)
                    act.wait_ge(s_tp, n)
                    act.activation(AT[:, slot, b * AB:(b + 1) * AB, bass.ds(k, 1), :].rearrange("p a o c -> p a (o c)"),
                                   bank[2 + b % TB][:, :].bitcast(F16)[:, 0:AB * P].rearrange("p (a c) -> p a c", a=AB),
                                   ACT.Copy).then_inc(s_tc, 1)
                    if ab is not None and b in AFTER_BATCH:
                        aggregate(AFTER_BATCH[b])

            act.wait_ge(s_rounds, 1)
            R = act.value_load(roundsI[0:1, 0:1], min_val=1, max_val=MAXR)
            with act.Fori(0, R) as r:
                blocks(act, r, step)

            act.wait_ge(s_var, 2)
            act.activation(lt2[:], lt1[:], ACT.Sqrt).then_inc(s_std, 1)
            with act.Fori(0, NT // 5) as i:
                for q in range(5):
                    t = i * 5 + q
                    act.wait_ge(s_tr, NT + t + 1 + HR)
                    act.wait_ge(s_xlo, t + 1)
                    act.activation(xT[:, q, :, :], row_slot(q).rearrange("p (k n) -> p k n", k=KD),
                                   ACT.Copy).then_inc(s_xT, 1)
                    act.activation(x2[:, 0, :, bass.ds(t * P, P)], row_slot(q).rearrange("p (k n) -> p k n", k=KD),
                                   ACT.Copy, scale=XUP).then_inc(s_xhi, 1)
            act.wait_ge(s_ex, 1)
            act.activation(probs[:], logits[:], ACT.Exp).then_inc(s_exd, 1)

            def split_weights(e, slot):
                act.activation(b1e[:, slot, :], b1T[:, :, bass.ds(e, 1)].rearrange("p f e -> p (f e)"),
                               ACT.Copy).then_inc(s_b1e, 1)
                act.activation(hup[:, slot, :], spread[:, 1, bass.ds(e, 1)], ACT.Copy).then_inc(s_b1e, 1)
                act.activation(gel[:, slot, :], gdown[:, bass.ds(e, 1)], ACT.Copy).then_inc(s_b1e, 1)
                for o in range(2):
                    act.activation(wup[:, slot, o:o + 1], spread[:, 0, bass.ds(e + o * NE, 1)], ACT.Copy).then_inc(s_b1e, 1)
                act.wait_ge(s_b1e, e * 5 + 5)
                for o in range(2):
                    act.activation(wparts[:, slot, 0, o, :], wf[:, bass.ds(e, 1), o, :].rearrange("p a w -> p (a w)"),
                                   ACT.Copy, scale=wup[:, slot, o:o + 1]).then_inc(s_whi, 1)

            act.wait_ge(s_es, 1)
            act.wait_ge(s_ew, 16 * 2 * NE)
            split_weights(0, 0)
            for b in range(CTB):
                act.wait_ge(s_cT, b + 1)
                n = min(4, NT - 4 * b) * P
                act.activation(cT[:, b * 4 * P:b * 4 * P + n], bank[b][0:NE, 0:n], ACT.Copy).then_inc(s_cTc, 1)

            def expert_pair(i, last_pair):
                for m in range(2 * NB):
                    def first_part(u):
                        f, th = u // 2, u % 2
                        act.wait_ge(s_gelu, i * (8 * NB) + (m * 4 + u + 1 + 4))
                        act.activation(hid[:, 0, m % 2, f, th * HALFC:(th + 1) * HALFC], hidf[:, u, :],
                                       ACT.Copy, scale=hup[:, m // NB, :]).then_inc(s_hhi, 1)

                    if m % NB == 0:
                        act.wait_ge(s_wlo, i * 4 + (m // NB * 2 + 2))
                    act.wait_ge(s_y, i * (2 * NT) + (m * BT + BT))
                    for u in range(4):
                        act.wait_ge(s_hid, i * (8 * NB) + (m * 4 + u + 1))
                        act.wait_ge(s_hlo, i * (8 * NB) + (m * 4 + u + 1))
                        act.activation(hidf[:, u, :], bank[u][:, 0:HALFC], ACT.Gelu,
                                       bias=b1e[:, m // NB, u // 2:u // 2 + 1],
                                       scale=gel[:, m // NB, :]).then_inc(s_gelu, 1)
                        if u:
                            first_part(u - 1)
                    first_part(3)
                    if m == 1:
                        split_weights(i * 2 + 1, 1)
                    if m == NB + 1 and not last_pair:
                        split_weights(i * 2 + 2, 0)

            with act.Fori(0, NE // 2 - 1) as i:
                expert_pair(i, False)
            expert_pair(NE // 2 - 1, True)

        @block.vector
        def _(dve):
            dve.sem_inc(s_yd, AR)
            dve.sem_inc(s_hc, HR)
            dve.sem_inc(s_xlo, HR)
            dve.sem_inc(s_hlo, 4)
            count = [0]

            def link(ins):
                count[0] += 1
                ins.then_inc(s_v, 1)
                dve.wait_ge(s_v, count[0])

            dve.wait_ge(s_edges, 96)
            dve.tensor_copy(fdst[:], edst[:])
            link(dve.tensor_copy(fsrc[:], esrc[:]))
            dve.scalar_tensor_tensor(eval_[:], fdst[:], float(NP), fsrc[:], ALU.mult, ALU.add).then_inc(s_val, 1)
            dve.wait_ge(s_val, 1)
            dve.tensor_reduce(chmax[:], eval_[:].rearrange("p (q e) -> p q e", q=EQ), AXX, ALU.max).then_inc(s_val, 1)
            L = EQ * P - 1
            link(dve.tensor_tensor(wide[0:EC, 0:L], fdst[:, 0:L], fdst[:, 1:L + 1], ALU.is_gt))
            link(dve.tensor_reduce(unsorted[:], wide[0:EC, 0:L], AXX, ALU.add))
            dve.wait_ge(s_row, 1)
            link(dve.tensor_copy(rowm[:].rearrange("o (p q) -> o q p", q=EQ),
                                 bank[0][0:1, 0:NCH].rearrange("o (q p) -> o q p", q=EQ)))
            dve.tensor_tensor_scan(rowp[:], rowm[:], rowm[:], 0.0, ALU.max, ALU.max).then_inc(s_mrow, 1)
            dve.wait_ge(s_mb, 1)
            dve.wait_ge(s_const, CONSTS)
            link(dve.tensor_scalar(thr[:], thrg[:], float(GROUP * NP), None, ALU.mult))
            for h in range(2):
                link(dve.tensor_scalar(cmpb[0:HG, :], bank[1][0:HG, 0:NCH], thr[0:HG, h:h + 1], None, ALU.is_lt))
                link(dve.tensor_reduce(cg[0:HG, h:h + 1], cmpb[0:HG, :], AXX, ALU.add))
            dve.tensor_copy(cgI[0:HG, :], cg[0:HG, :]).then_inc(s_cg, 1)

            dve.wait_ge(s_w, 48)
            dve.tensor_reduce(wmax[:, 0:1], Wsb.rearrange("p h c -> p (h c)"), AXX, ALU.max).then_inc(s_wmax, 1)
            dve.tensor_reduce(wmax[:, 1:2], Wsb.rearrange("p h c -> p (h c)"), AXX, ALU.min).then_inc(s_wmax, 1)
            dve.tensor_reduce(bmax[0:NE, 0:1], b1s, AXX, ALU.max)
            link(dve.tensor_reduce(bmax[0:NE, 1:2], b1s, AXX, ALU.min))
            link(dve.tensor_scalar(bmax[0:NE, 1:2], bmax[0:NE, 1:2], -1.0, None, ALU.mult))
            link(dve.tensor_tensor(bmax[0:NE, 0:1], bmax[0:NE, 0:1], bmax[0:NE, 1:2], ALU.max))

            dve.wait_ge(s_srcT, 1)
            link(dve.tensor_copy(srcI[:], bank[2][:, 0:NCH]))
            dve.tensor_scalar(lowI[:], srcI[:], P - 1, None, ALU.bitwise_and)
            link(dve.tensor_scalar(highI[:], srcI[:], 7, None, ALU.arith_shift_right))
            dve.tensor_copy(lowh[:], lowI[:])
            link(dve.tensor_copy(highh[:], highI[:]))
            for j in range(NT):
                dve.tensor_scalar(highhot[:, j, :], highh[:], iotaf[:, j:j + 1], None, ALU.is_equal).then_inc(s_hots, 1)
            dve.wait_ge(s_wrow, 1)
            dve.tensor_reduce(wtop[:, 0:1], bank[3][0:1, 0:P], AXX, ALU.max)
            link(dve.tensor_reduce(wtop[:, 1:2], bank[3][0:1, P:2 * P], AXX, ALU.min))
            link(dve.tensor_scalar(wtop[:, 1:2], wtop[:, 1:2], -1.0, None, ALU.mult))
            link(dve.tensor_tensor(wtop[:, 0:1], wtop[:, 0:1], wtop[:, 1:2], ALU.max))
            link(dve.tensor_scalar(wexp[:], wtop[:, 0:1].bitcast(I32), 23, None, ALU.arith_shift_right))
            link(dve.tensor_copy(wtop[:, 1:2], wexp[:]))
            link(dve.tensor_scalar(wtop[:, 2:3], wtop[:, 1:2], -1.0, FEATURE_EXP, ALU.mult, ALU.add))
            link(dve.tensor_scalar(wtop[:, 2:3], wtop[:, 2:3], 253.0, float(1 << 23), ALU.min, ALU.mult))
            link(dve.tensor_scalar(wtop[:, 3:4], wtop[:, 2:3], -1.0, 254.0 * (1 << 23), ALU.mult, ALU.add))
            dve.tensor_copy(wpow[:], wtop[:, 2:4]).then_inc(s_ws, 1)
            with dve.Fori(0, P // 32) as i:
                for u in range(32):
                    j = i * 32 + u
                    dve.tensor_scalar(lowhot[:, bass.ds(j, 1), :].rearrange("p o c -> p (o c)"), lowh[:],
                                      iotaf[:, bass.ds(j, 1)], None, ALU.is_equal).then_inc(s_hots, 1)

            dve.wait_ge(s_wb, 1)
            link(dve.tensor_copy(scaleb[:], bank[4][:, 0:2]))

            dve.wait_ge(s_grow, 32)
            for h in range(2):
                link(dve.tensor_tensor_scan(gscan[0:HG, h, :], grow[0:HG, h, :], grow[0:HG, h, :], 0.0, ALU.max, ALU.max))
                link(dve.tensor_scalar(cmpb[0:HG, 0:P], gscan[0:HG, h, :], thr[0:HG, h:h + 1], None, ALU.is_lt))
                link(dve.tensor_reduce(ng[0:HG, h:h + 1], cmpb[0:HG, 0:P], AXX, ALU.add))
            dve.scalar_tensor_tensor(start[0:HG, :], cg[0:HG, :], float(P), ng[0:HG, :], ALU.mult, ALU.add).then_inc(s_start, 1)
            dve.wait_ge(s_start, 1)
            link(dve.tensor_copy(startc[0:HG, :], start[0:HG, :]))
            dve.tensor_copy(startI[0:HG, :], startc[0:HG, :]).then_inc(s_idx, 1)
            dve.wait_ge(s_strow, 1)
            link(dve.tensor_copy(bound[:], bank[0][0:1, 0:NG + 3 * EC]))
            link(dve.tensor_tensor(diff[:, 0:NG - 1], bound[:, 1:NG], bound[:, 0:NG - 1], ALU.subtract))
            dve.tensor_reduce(small[:, 0:1], diff[:, 0:NG - 1], AXX, ALU.max)
            link(dve.tensor_tensor(rowm[:, 0:EC - 1], bound[:, NG:NG + EC - 1], bound[:, NG + EC + 1:NG + 2 * EC], ALU.is_gt))
            dve.tensor_reduce(small[:, 1:2], rowm[:, 0:EC - 1], AXX, ALU.add)
            link(dve.tensor_reduce(small[:, 2:3], bound[:, NG + 2 * EC:NG + 3 * EC], AXX, ALU.add))
            link(dve.tensor_tensor(small[:, 3:4], small[:, 1:2], small[:, 2:3], ALU.add))
            link(dve.tensor_scalar(small[:, 4:5], small[:, 3:4], 0.0, float(EP), ALU.is_gt, ALU.mult))
            link(dve.tensor_tensor(small[:, 5:6], small[:, 4:5], small[:, 0:1], ALU.max))
            link(dve.tensor_scalar(kcmp[:], kwin[:], small[:, 5:6], None, ALU.is_lt))
            link(dve.tensor_reduce(small[:, 6:7], kcmp[:], AXX, ALU.add))
            link(dve.tensor_scalar(small[:, 7:8], small[:, 6:7], 1.0, None, ALU.max))
            dve.tensor_copy(roundsI[:], small[:, 7:8]).then_inc(s_rounds, 1)

            def layernorm_root(base):
                dve.wait_ge(s_std, base + 1)
                link(dve.reciprocal(rstd[:], lt2[:]))

            def layernorm_second():
                dve.wait_ge(s_stat, NT)
                me, mo, ve, vo = (stats[:, :, c] for c in (1, 4, 2, 5))
                dve.tensor_tensor(lt1[:], me, mo, ALU.add)
                link(dve.tensor_tensor(lt2[:], me, mo, ALU.subtract))
                dve.tensor_scalar(mean[:], lt1[:], 0.5, None, ALU.mult)
                dve.tensor_tensor(rstd[:], ve, vo, ALU.add)
                link(dve.scalar_tensor_tensor(lt3[:], lt2[:], 0.25, lt2[:], ALU.mult, ALU.mult))
                link(dve.scalar_tensor_tensor(lt2[:], rstd[:], 1.0 / D, lt3[:], ALU.mult, ALU.add))
                dve.tensor_scalar(lt1[:], lt2[:], EPS, None, ALU.add).then_inc(s_var, 1)
                layernorm_root(1)

            def normalise(base, i, q):
                t = i * 5 + q
                dve.wait_ge(s_tr, base * NT + t + 1)
                if base:
                    dve.wait_ge(s_x2, t + 1)
                xt = X[:, bass.ds(t, 1), :].rearrange("p o d -> p (o d)")
                dve.tensor_scalar(xn[:, q, :], xt, mean[:, bass.ds(t, 1)], rstd[:, bass.ds(t, 1)],
                                  ALU.subtract, ALU.mult).then_inc(s_xn, 1)

            def split_features(i, q):
                t = i * 5 + q
                dve.wait_ge(s_hself, t + 1 + HR)
                part = H[:, :, bass.ds(t, 1), :].rearrange("p s o d -> p s (o d)")
                dve.scalar_tensor_tensor(part[:, 1, :], feat_slot(q), rsup[:, bass.ds(t, 1)], part[:, 0, :],
                                         ALU.mult, ALU.subtract).then_inc(s_hc, 1)

            dve.wait_ge(s_var, 1)
            dve.tensor_scalar(mean[:], lt3[:], -1.0, None, ALU.mult)
            layernorm_root(0)
            dve.wait_ge(s_sqrt, 1)
            link(dve.reciprocal(rs[:], deg[:]))
            dve.tensor_tensor(rs2[:], rs[:], rs[:], ALU.mult)
            dve.tensor_scalar(rsdown[:], rs[:], scaleb[:, 1:2], None, ALU.mult)
            dve.tensor_scalar(rsup[:], rs[:], scaleb[:, 0:1], None, ALU.mult).then_inc(s_rs, 1)
            dve.wait_ge(s_rs, 1)
            for q in range(5):
                normalise(0, 0, q)
            with dve.Fori(0, NT // 5 - 1) as i:
                for q in range(5):
                    split_features(i, q)
                    normalise(0, i + 1, q)
            for q in range(5):
                split_features(NT // 5 - 1, q)

            R = dve.value_load(roundsI[0:1, 0:1], min_val=1, max_val=MAXR)
            KR = 3

            with dve.Fori(0, R) as r:
                def rlink(ins, n):
                    ins.then_inc(s_vr, 1)
                    dve.wait_ge(s_vr, r * KR + n)

                rlink(dve.tensor_scalar(startc[0:HG, :], startc[0:HG, :], float(WIN), float(EP), ALU.add, ALU.min), 1)
                dve.wait_ge(s_wg, r * 32 + 32)
                dve.tensor_copy(startI[0:HG, :], startc[0:HG, :]).then_inc(s_idx, 1)
                dve.wait_ge(s_wt, r + 1)
                dve.tensor_copy(winI[:, 0:2, :], bank[2][:, 0:2 * NG].rearrange("p (j g) -> p j g", j=2))
                rlink(dve.tensor_copy(winI[:, 2:3, :], bank[3][:, 0:NG].rearrange("p (j g) -> p j g", j=1)), 2)
                dve.tensor_scalar(lowwI[:], winI[:], P - 1, None, ALU.bitwise_and)
                rlink(dve.tensor_scalar(keywI[:], winI[:], 7, None, ALU.arith_shift_right), 3)
                dve.tensor_copy(lowk[:], lowwI[:])
                dve.tensor_tensor(key[:], keywI[:], gbase[:], ALU.subtract).then_inc(s_key, 1)
                dve.wait_ge(s_sqrt, 1)
                dve.wait_ge(s_key, r + 1)
                with dve.Fori(0, NT) as t:
                    for g in range(GPT):
                        col = t * GPT + g
                        dve.wait_ge(s_cnt, r * NG + t * GPT + (g + 1))
                        for j in range(J):
                            dve.tensor_scalar(hotlow[:, g % RING, j, :], iotah[:], lowk[:, j, bass.ds(col, 1)],
                                              None, ALU.is_equal)
                            last = dve.tensor_scalar(hotkey[:, g % RING, j, :], keytab[:].rearrange("p a d -> p (a d)"),
                                                     key[:, j, bass.ds(col, 1)], None, ALU.is_equal)
                        last.then_inc(s_hot, 1)

            pieces = [(ALU.max, 0, 0), (ALU.max, 0, 1), (ALU.min, 1, 0), (ALU.min, 1, 1)]
            for a in range(NT // 5):
                dve.wait_ge(s_aa, R * AGR + (a * 5 + 5 + AR))
                for t in range(a * 5, a * 5 + 5):
                    dve.bn_stats(stats[:, t, :], X[:, t, :]).then_inc(s_stat, 1)
                if a < len(pieces):
                    op, m, o = pieces[a]
                    dve.wait_ge(s_ew, 16 * 2 * NE)
                    last = dve.tensor_reduce(emax[:, m, o * NE:(o + 1) * NE], wf[:, :, o, :], AXX, op)
                    if a == len(pieces) - 1:
                        link(last)
            link(dve.tensor_scalar(emax[:, 1, :], emax[:, 1, :], -1.0, None, ALU.mult))
            dve.tensor_tensor(emax[:, 0, :], emax[:, 0, :], emax[:, 1, :], ALU.max).then_inc(s_emax, 1)
            dve.wait_ge(s_round_end, 1)
            layernorm_second()

            def second_part(i, q):
                t = i * 5 + q
                dve.wait_ge(s_xhi, t + 1 + HR)
                dve.scalar_tensor_tensor(x2[:, 1, :, bass.ds(t * P, P)], xT[:, q, :, :], XUP,
                                         x2[:, 0, :, bass.ds(t * P, P)], ALU.mult, ALU.subtract).then_inc(s_xlo, 1)

            for q in range(5):
                normalise(1, 0, q)
            with dve.Fori(0, NT // 5 - 1) as i:
                for q in range(5):
                    second_part(i, q)
                    normalise(1, i + 1, q)
            for q in range(5):
                second_part(NT // 5 - 1, q)
            dve.wait_ge(s_erow, 1)
            link(dve.tensor_reduce(etop[:, 0:1], bank[5][0:2 * NE, 0:P], AXX, ALU.max))
            link(dve.scalar_tensor_tensor(etop[:, 1:2], etop[:, 0:1], float(D), bmax[:, 0:1], ALU.mult, ALU.add))
            link(dve.tensor_scalar(eexp[:], etop[:, 0:2].bitcast(I32), 23, None, ALU.arith_shift_right))
            link(dve.tensor_copy(etop[:, 2:4], eexp[:]))
            link(dve.tensor_scalar(etop[:, 2:4], etop[:, 2:4], -1.0, BOUND_EXP, ALU.mult, ALU.add))
            link(dve.tensor_scalar(etop[:, 0:2], etop[:, 2:4], 253.0, float(1 << 23), ALU.min, ALU.mult))
            link(dve.tensor_scalar(etop[:, 2:4], etop[:, 0:2], -1.0, 254.0 * (1 << 23), ALU.mult, ALU.add))
            link(dve.tensor_copy(epow[:], etop[:]))
            for c in range(4):
                last = dve.tensor_scalar(ediag[:, c, :], identf[0:2 * NE, 0:2 * NE], epow[:, c:c + 1].bitcast(F32),
                                         None, ALU.mult)
            last.then_inc(s_epow, 1)
            dve.wait_ge(s_lg, 1)
            link(dve.tensor_copy(logits[:], bank[7][:, 0:NT * NE].rearrange("p (t e) -> p t e", t=NT)))
            link(dve.tensor_reduce(rowr[:], logits[:], AXX, ALU.max))
            wide8 = lambda a: a.unsqueeze(2).to_broadcast([P, NT, NE])
            dve.tensor_tensor(logits[:], logits[:], wide8(rowr[:]), ALU.subtract).then_inc(s_ex, 1)
            dve.wait_ge(s_espread, 1)
            link(dve.tensor_copy(spread[:], bank[6][:, 0:4 * 2 * NE].rearrange("p (c e) -> p c e", c=4)))
            dve.tensor_tensor(ydown[:], spread[:, 3, 0:NE], spread[:, 2, NE:2 * NE], ALU.mult)
            dve.tensor_scalar(gdown[:], spread[:, 2, 0:NE], 1.0 / XUP, None, ALU.mult).then_inc(s_es, 1)
            dve.wait_ge(s_es, 1)
            dve.wait_ge(s_exd, 1)
            link(dve.tensor_reduce(rowr[:], probs[:], AXX, ALU.add))
            link(dve.reciprocal(lt1[:], rowr[:]))
            link(dve.tensor_tensor(probs[:], probs[:], wide8(lt1[:]), ALU.mult))
            for t in range(NT):
                last = dve.max(top[:, t, :], probs[:, t, :])
            link(last)
            for t in range(NT):
                last = dve.max_index(topi[:, t, :], top[:, t, :], probs[:, t, :])
            link(last)
            link(dve.tensor_copy(topf[:], topi[:, :, 0:2]))
            link(dve.tensor_tensor(lt1[:], top[:, :, 0], top[:, :, 1], ALU.add))
            link(dve.tensor_scalar(lt2[:], lt1[:], 1e-12, None, ALU.max))
            dve.reciprocal(rowr[:], lt2[:])
            dve.tensor_tensor(hot1[:], iota8[:], wide8(topf[:, :, 0]), ALU.is_equal)
            link(dve.tensor_tensor(hot2[:], iota8[:], wide8(topf[:, :, 1]), ALU.is_equal))
            link(dve.tensor_tensor(hot1[:], hot1[:], hot2[:], ALU.add))
            link(dve.tensor_tensor(hot1[:], hot1[:], probs[:], ALU.mult))
            dve.tensor_tensor(comb[:], hot1[:], wide8(rowr[:]), ALU.mult).then_inc(s_comb, 1)
            dve.wait_ge(s_comb, 1)
            dve.tensor_tensor(combs[:], comb[:], ydown[:].unsqueeze(1).to_broadcast([P, NT, NE]), ALU.mult)

            def second_weights(e, slot):
                for o in range(2):
                    dve.wait_ge(s_whi, e * 2 + (o + 1))
                    dve.scalar_tensor_tensor(wparts[:, slot, 1, o, :], wf[:, bass.ds(e, 1), o, :].rearrange("p a w -> p (a w)"),
                                             wup[:, slot, o:o + 1], wparts[:, slot, 0, o, :],
                                             ALU.mult, ALU.subtract).then_inc(s_wlo, 1)

            second_weights(0, 0)
            dve.wait_ge(s_x2, NT + HR)
            for b in range(YB):
                dve.wait_ge(s_bias, b + 1)
                n = min(2, NT - 2 * b)
                dve.tensor_tensor(X[:, 2 * b:2 * b + n, :], X[:, 2 * b:2 * b + n, :],
                                  bank[b % 7][:, 0:n * D].rearrange("p (t d) -> p t d", d=D), ALU.add).then_inc(s_biasd, 1)
            dve.wait_ge(s_biasd, YB)

            def expert_pair(i, last_pair):
                def second_hidden(m, u):
                    f, th = u // 2, u % 2
                    dve.wait_ge(s_hhi, i * (8 * NB) + (m * 4 + u + 1))
                    part = hid[:, :, m % 2, f, th * HALFC:(th + 1) * HALFC]
                    dve.scalar_tensor_tensor(part[:, 1, :], hidf[:, u, :], hup[:, m // NB, :], part[:, 0, :],
                                             ALU.mult, ALU.subtract).then_inc(s_hlo, 1)

                def add(m, q):
                    dve.wait_ge(s_y, i * (2 * NT) + (m * BT + q + 1 + FREE_Y))
                    t = (m % NB) * BT + q
                    dve.scalar_tensor_tensor(X[:, t, :], half_slot(q),
                                             combs[:, t, bass.ds(i * 2 + m // NB, 1)], X[:, t, :],
                                             ALU.mult, ALU.add).then_inc(s_yd, 1)

                for u in range(4):
                    second_hidden(0, u)
                for m in range(2 * NB):
                    if m == 1:
                        second_weights(i * 2 + 1, 1)
                    if m == NB + 1 and not last_pair:
                        second_weights(i * 2 + 2, 0)
                    for u in range(3):
                        if m + 1 < 2 * NB:
                            second_hidden(m + 1, u)
                    add(m, 0)
                    if m + 1 < 2 * NB:
                        second_hidden(m + 1, 3)
                    for q in range(1, BT):
                        add(m, q)

            with dve.Fori(0, NE // 2 - 1) as i:
                expert_pair(i, False)
            expert_pair(NE // 2 - 1, True)

        @block.tensor
        def _(pe):
            mm = pe.matmul
            pe.sem_inc(s_cnt, RING)
            pe.sem_inc(s_tr, HR)
            pe.sem_inc(s_y, FREE_Y)
            pe.wait_ge(s_const, CONSTS)
            pe.wait_ge(s_val, 2)
            for q in range(EQ):
                last = mm(bank[0][0:1, q * EC:(q + 1) * EC], chmax[:, q:q + 1], identf[0:EC, 0:EC], start=True, stop=True)
            last.then_inc(s_row, 1)
            for q in range(EQ):
                last = pe.transpose(bank[2][:, q * EC:(q + 1) * EC], fsrc[:, q * P:(q + 1) * P], identf[0:EC, 0:EC])
            last.then_inc(s_srcT, 1)
            pe.wait_ge(s_mrow, 1)
            mm(bank[1][:, 0:NCH], ones[0:1, :], rowp[:], start=True, stop=True).then_inc(s_mb, 1)
            pe.wait_ge(s_w, 48)
            for k in range(KD):
                for h in range(KD):
                    pe.transpose(bank[5][:, k * D + h * P:k * D + (h + 1) * P], Wsb[:, h, k * P:(k + 1) * P], identf[:])
            for k in range(KD):
                pe.transpose(bank[6][:, k * NE:(k + 1) * NE], rw[:, k * P:(k + 1) * P], identf[0:NE, 0:NE])
                last = pe.transpose(bank[6][:, 64 + k * NE:64 + (k + 1) * NE], b1s[:, k * P:(k + 1) * P], identf[0:NE, 0:NE])
            last.then_inc(s_wT, 1)
            pe.wait_ge(s_wmax, 2)
            for m in range(2):
                last = mm(bank[3][0:1, m * P:(m + 1) * P], wmax[:, m:m + 1], identf[:], start=True, stop=True)
            last.then_inc(s_wrow, 1)
            pe.wait_ge(s_ws, 1)
            mm(bank[4][:, 0:2], ones[0:1, :], wpow[:].bitcast(F32), start=True, stop=True).then_inc(s_wb, 1)
            pe.wait_ge(s_start, 1)
            for h in range(2):
                mm(bank[0][0:1, h * HG:(h + 1) * HG], start[0:HG, h:h + 1], identf[0:HG, 0:HG], start=True, stop=True)
            for n, col in enumerate((fdst[:, EQ * P - 1:EQ * P], fdst[:, 0:1], unsorted[:])):
                last = mm(bank[0][0:1, NG + n * EC:NG + (n + 1) * EC], col, identf[0:EC, 0:EC], start=True, stop=True)
            last.then_inc(s_strow, 1)
            pe.wait_ge(s_hots, NT + P)
            mm(bank[7][:, 0:NT], zerosh[:], zerosh[:, 0:NT], start=True, stop=False)
            for c in range(NCH):
                mm(bank[7][:, 0:NT], lowhot[:, :, c], highhot[:, :, c], start=False, stop=False)
            mm(bank[7][:, 0:NT], zerosh[:], zerosh[:, 0:NT], start=False, stop=True).then_inc(s_deg, 1)

            def transpose_rows(base, i, q):
                pe.wait_ge(s_xn, base * NT + i * 5 + (q + 1))
                for k in range(KD):
                    last = pe.transpose(row_slot(q)[:, k * P:(k + 1) * P], xn[:, q, k * P:(k + 1) * P], identf[:])
                last.then_inc(s_tr, 1)

            def rows(i, q):
                pe.wait_ge(s_hc, i * 5 + (q + 1))
                transpose_rows(0, i, q)

            def features(i, q):
                pe.wait_ge(s_xT, i * 5 + (q + 1))
                for k in range(KD):
                    last = mm(feat_slot(q), xT[:, q, k, :], WT[:, k, :], start=(k == 0), stop=(k == KD - 1))
                last.then_inc(s_h, 1)

            pe.wait_ge(s_wTc, 3)
            pe.wait_ge(s_rounds, 1)
            pe.wait_ge(s_wb, 1)
            feature_loop(pe, rows, features)

            def step(r, k, bb, slot, ab, aslot):
                def aggregate(q):
                    n = r * AGR + ab * NT + k * BT + (q + 1)
                    pe.wait_ge(s_ac, n + EARLIER[q])
                    for j in range(BT):
                        for s in range(2):
                            last = mm(half_slot(q),
                                      AT[:, aslot, bass.ds(k * BT + q, 1), j, :].rearrange("p o c -> p (o c)"),
                                      H[:, s, bass.ds(ab * BT + j, 1), :].rearrange("p o d -> p (o d)"),
                                      start=(j == 0 and s == 0), stop=(j == BT - 1 and s == 1))
                    last.then_inc(s_ag, 1)

                if ab is not None:
                    pe.wait_ge(s_tc, r * TPR + ab * NT + (NT + TB))
                if bb is None:
                    for q in range(BT):
                        aggregate(q)
                    return
                for g in range(GPT):
                    n = r * NG + bb * (BT * GPT) + k * GPT + (g + 1)
                    pe.wait_ge(s_hot, n)
                    pe.wait_ge(s_cc, n)
                    for j in range(J):
                        last = mm(bank[g % CB][:, 0:COLS], hotlow[:, g % RING, j, :], hotkey[:, g % RING, j, :],
                                  start=(j == 0), stop=(j == J - 1))
                    last.then_inc(s_cnt, 1)
                    if ab is not None and g in AFTER_GROUP:
                        aggregate(AFTER_GROUP[g])
                pe.wait_ge(s_cc, r * NG + bb * (BT * GPT) + k * GPT + (GPT + CB))
                for b in range(BT):
                    n = r * TPR + bb * NT + k * BT + (b + 1)
                    pe.wait_ge(s_tc, n + (1 if b == 0 else 0))
                    for u in range(AB):
                        last = pe.transpose(bank[2 + b % TB][:, :].bitcast(F16)[:, u * P:(u + 1) * P],
                                            CNT[:, b * AB + u, :], identh[:])
                    last.then_inc(s_tp, 1)
                    if ab is not None and b in AFTER_BATCH:
                        aggregate(AFTER_BATCH[b])

            pe.wait_ge(s_hc, NT + HR)
            R = pe.value_load(roundsI[0:1, 0:1], min_val=1, max_val=MAXR)
            with pe.Fori(0, R) as r:
                pe.wait_ge(s_wg, r * 32 + 32)
                pe.wait_ge(s_tc, r * TPR + TB)
                for j in range(J):
                    for h in range(2):
                        c = (j % 2) * NG + h * HG
                        last = pe.transpose(bank[2 + j // 2][:, c:c + HG], wrows[0:HG, h, j * P:(j + 1) * P],
                                            identf[0:HG, 0:HG])
                last.then_inc(s_wt, 1)
                blocks(pe, r, step)

            def route(i, q):
                pe.wait_ge(s_xT, NT + i * 5 + (q + 1))
                for k in range(KD):
                    last = mm(bank[7][:, bass.ds(i * (5 * NE) + q * NE, NE)], xT[:, q, k, :], rwT[:, k, :],
                              start=(k == 0), stop=(k == KD - 1))
                last.then_inc(s_lg1, 1)

            pe.wait_ge(s_round_end, 1)
            pe.wait_ge(s_emax, 1)
            mm(bank[5][0:2 * NE, 0:P], emax[:, 0, :], identf[:], start=True, stop=True).then_inc(s_erow, 1)
            feature_loop(pe, lambda i, q: transpose_rows(1, i, q), route)
            mm(bank[6][:, 0:8], zerosh[:], zerosh[:, 0:8], start=True, stop=True).then_inc(s_lg, 1)
            pe.wait_ge(s_epow, 1)
            mm(bank[6][:, 0:8 * NE], ones[:], ediag[:].rearrange("p c e -> p (c e)"),
               start=True, stop=True).then_inc(s_espread, 1)
            pe.wait_ge(s_comb, 1)
            for t in range(NT):
                last = pe.transpose(bank[t // 4][0:NE, t % 4 * P:(t % 4 + 1) * P], comb[:, t, :], identf[:])
                if t % 4 == 3 or t == NT - 1:
                    last.then_inc(s_cT, 1)
            pe.wait_ge(s_b2, 16)
            for b in range(YB):
                if b < 7:
                    pe.wait_ge(s_cTc, CTB if b == 0 else CTB)
                else:
                    pe.wait_ge(s_biasd, b - 6)
                for t in range(2 * b, min(2 * b + 2, NT)):
                    last = mm(bank[b % 7][:, t % 2 * D:(t % 2 + 1) * D], cT[:, t * P:(t + 1) * P], b2s[:],
                              start=True, stop=True)
                last.then_inc(s_bias, 1)

            PARTS = ((0, 0), (0, 1), (1, 0))

            def hidden(i, m):
                slot, c = m // NB % 2, m % NB
                if c == 0:
                    pe.wait_ge(s_wlo, i * 4 + (m // NB * 2 + 2))
                for u in range(4):
                    f, th = u // 2, u % 2
                    pe.wait_ge(s_gelu, i * (8 * NB) + (m * 4 + u + 1))
                    for k in range(KD):
                        for a, (sw, sx) in enumerate(PARTS):
                            last = mm(bank[u][:, 0:HALFC],
                                      wparts[:, slot, sw, 0, k * D + f * P:k * D + (f + 1) * P],
                                      x2[:, sx, k, c * BT * P + th * HALFC:c * BT * P + (th + 1) * HALFC],
                                      start=(k == 0 and a == 0), stop=(k == KD - 1 and a == 2))
                    last.then_inc(s_hid, 1)

            def outputs(i, m):
                slot = m // NB
                pe.wait_ge(s_hlo, i * (8 * NB) + (m * 4 + 4 + 4))
                for q in range(BT):
                    pe.wait_ge(s_yd, i * (2 * NT) + (m * BT + q + 1 + EARLIER[q]))
                    for k in range(KD):
                        for a, (sh, sw) in enumerate(PARTS):
                            last = mm(half_slot(q), hid[:, sh, m % 2, k, q * P:(q + 1) * P],
                                      wparts[:, slot, sw, 1, k * D:(k + 1) * D],
                                      start=(k == 0 and a == 0), stop=(k == KD - 1 and a == 2))
                    last.then_inc(s_y, 1)

            def expert_pair(i, last_pair):
                for m in range(2 * NB):
                    if m + 1 < 2 * NB or not last_pair:
                        hidden(i, m + 1)
                    outputs(i, m)

            pe.wait_ge(s_biasd, YB)
            hidden(0, 0)
            with pe.Fori(0, NE // 2 - 1) as i:
                expert_pair(i, False)
            expert_pair(NE // 2 - 1, True)


_INS = ["x", "src", "dst", "L0_gnn_W", "L0_ffn_router_w", "L0_ffn_w1", "L0_ffn_b1", "L0_ffn_w2", "L0_ffn_b2"]


def kernel(**inputs):
    import numpy as _np
    import concourse.bacc as _bacc
    from concourse import mybir as _mybir
    from concourse.bass_utils import run_bass_kernel_spmd as _run

    nc = _bacc.Bacc("TRN2", target_bir_lowering=False, num_devices=1)
    arrays, args = {}, []
    for name in _INS:
        a = _np.ascontiguousarray(inputs[name])
        arrays[f"in_{name}"] = a
        args.append(nc.dram_tensor(f"in_{name}", a.shape, _mybir.dt.from_np(a.dtype), kind="ExternalInput").ap())
    shape = inputs["x"].shape
    args.append(nc.dram_tensor("out", shape, _mybir.dt.float32, kind="ExternalOutput").ap())
    gnn_moe(nc, *args)
    r = _run(nc, [arrays], core_ids=[0])
    return r.results[0]["out"]
```
